# Optimizing a Trainium2 kernel written in Bass

```python
import numpy as np
import jax
import jax.numpy as jnp

def _softmax(x, axis=-1):
    return jax.nn.softmax(x, axis=axis)
def _gelu(x):
    return jax.nn.gelu(x, approximate=True)
def _silu(x):
    return jax.nn.silu(x)
def _sigmoid(x):
    return jax.nn.sigmoid(x)
def _layernorm(x, axis=-1, eps=1e-5):
    m = jnp.mean(x, axis=axis, keepdims=True)
    v = jnp.var(x, axis=axis, keepdims=True)
    return (x - m) / jnp.sqrt(v + eps)
def _scatter_add(tgt, idx, src, axis=0):
    return tgt.at[idx].add(src)
def _segment_sum(src, seg, n):
    return jax.ops.segment_sum(src, seg, n)

kernel_name = 'mk_adj_preln_d2_adj_64_4e852f'

def setup_inputs(seed: int = 0):
    np.random.seed(seed)
    _w = jnp.asarray
    def _rec_inputs():
        import jax
        import jax.numpy as jnp
        _gk = jax.random.key(seed)
        x = -0.000929 + 1 * jax.random.normal(jax.random.fold_in(_gk, 1), (8192, 64), jnp.float32)
        _a = jax.random.bernoulli(jax.random.fold_in(_gk, 2), 0.000488281, (8192, 8192))
        _a = jnp.logical_or(_a, jnp.swapaxes(_a, -1, -2))
        _a = jnp.logical_or(_a, jnp.eye(8192, dtype=bool))
        adj = _a.astype(jnp.int32)
        return x, adj
    x, adj = _rec_inputs()
    def _L0_gnn_setup():
        import jax, jax.numpy as jnp
        import numpy as np
        N = 16384
        D = 64
        key = jax.random.key(seed)
        kx, ka = jax.random.split(key)
        x = jax.random.normal(kx, (N, D), dtype=jnp.float32)
        adj = jax.random.randint(ka, (N, N), 0, 2, dtype=jnp.int32)
        return {'x': x, 'adj': adj}
    _L0_gnn_all = _L0_gnn_setup()
    _L0_gnn_in = {k: v for k, v in _L0_gnn_all.items() if k in ()}
    del _L0_gnn_all

    def _L1_gnn_setup():
        import jax, jax.numpy as jnp
        import numpy as np
        N = 12288
        IN_C = 64
        OUT_C = 64
        NEG_INF = -1000000000.0
        key = jax.random.key(seed)
        k1, k2, k3, k4 = jax.random.split(key, 4)
        x = jax.random.normal(k1, (N, IN_C), dtype=jnp.float32)
        edge_index = jax.random.randint(k2, (N, N), 0, 2, dtype=jnp.int32)
        weight_w = jax.random.normal(k3, (IN_C, OUT_C), dtype=jnp.float32) * (1.0 / np.sqrt(IN_C))
        weight_a = jax.random.normal(k4, (2 * OUT_C, 1), dtype=jnp.float32) * (1.0 / np.sqrt(OUT_C))
        bias = jnp.zeros((OUT_C,), dtype=jnp.float32)
        return {'x': x, 'edge_index': edge_index, 'weight_w': weight_w, 'weight_a': weight_a, 'bias': bias}
    _L1_gnn_all = _L1_gnn_setup()
    _L1_gnn_in = {k: v for k, v in _L1_gnn_all.items() if k in ('weight_w', 'weight_a', 'bias', )}
    del _L1_gnn_all

    return {
        "x": x,
        "adj": adj,
        "L1_gnn_weight_w": _L1_gnn_in["weight_w"],
        "L1_gnn_weight_a": _L1_gnn_in["weight_a"],
        "L1_gnn_bias": _L1_gnn_in["bias"],
    }

def reference(x, adj, L1_gnn_weight_w, L1_gnn_weight_a, L1_gnn_bias):
    import jax
    import jax.numpy as jnp
    def _L0_gnn_ref(x, adj):
        import jax, jax.numpy as jnp
        import numpy as np
        N = 16384
        D = 64
        a = (adj == 1).astype(x.dtype)
        return jnp.matmul(a, x) + x

    def _L1_gnn_ref(x, edge_index, weight_w, weight_a, bias):
        import jax, jax.numpy as jnp
        import numpy as np
        N = 12288
        IN_C = 64
        OUT_C = 64
        NEG_INF = -1000000000.0
        wh = x @ weight_w
        a_src = weight_a[:OUT_C, 0]
        a_dst = weight_a[OUT_C:, 0]
        e = (wh @ a_src)[:, None] + (wh @ a_dst)[None, :]
        e = jax.nn.leaky_relu(e, negative_slope=0.01)
        scores = jnp.where(edge_index > 0, e, NEG_INF)
        attention = jax.nn.softmax(scores, axis=1)
        out = attention @ wh
        return out + bias

    h = jnp.maximum(_layernorm(x, axis=-1), 0.0)
    x = x + _L0_gnn_ref(h, adj)
    h = jnp.maximum(_layernorm(x, axis=-1), 0.0)
    x = x + _L1_gnn_ref(h, adj, L1_gnn_weight_w, L1_gnn_weight_a, L1_gnn_bias)
    return x


_drawn_inputs = setup_inputs


def setup_inputs(seed=0):
    import zlib

    import numpy as np

    out = dict(_drawn_inputs(seed))
    spreads = {'L1_gnn_bias': (0.0, 0.405)}
    factors = {'L1_gnn_weight_a': 2.908}
    for name, (base, spread) in spreads.items():
        noise = np.random.default_rng([zlib.crc32(name.encode()), seed]).standard_normal(out[name].shape)
        drawn = base * np.exp(spread * noise) if base else spread * noise
        out[name] = jnp.asarray(drawn.astype(out[name].dtype))
    for name, factor in factors.items():
        out[name] = (out[name] * factor).astype(out[name].dtype)
    return out
```

```python
import concourse.bass as bass
import concourse.mybir as mybir
from contextlib import ExitStack

F32 = mybir.dt.float32
BF16 = mybir.dt.bfloat16
FP8 = mybir.dt.float8e4
I32 = mybir.dt.int32
I8 = mybir.dt.int8
U8 = mybir.dt.uint8
U16 = mybir.dt.uint16
U32 = mybir.dt.uint32
ALU = mybir.AluOpType
ACT = mybir.ActivationFunctionType
AXX = mybir.AxisListType.X
RMAX = bass.bass_isa.ReduceOp.max


def gnn_two_layers(
    nc: bass.Bass,
    x: bass.AP,
    adj: bass.AP,
    weight_w: bass.AP,
    weight_a: bass.AP,
    bias: bass.AP,
    out: bass.AP,
):
    N, D = x.shape
    P = 128
    T = N // P
    HALF = T // 2
    SUP = 4
    NS = T // SUP
    W4 = P // 8
    W1 = P // 16
    DE = D + 1
    SUPW = SUP * P
    CT = 16
    NCH = T // CT
    SAFE = 50.0
    SLOPE = 0.01
    EPS = 1e-5
    KB = 1024
    HEAD = 4

    def done(k):
        return k + HEAD

    ctx = ExitStack()
    with ctx:
        def sb(name, shape, dt):
            return ctx.enter_context(nc.sbuf_tensor(name, shape, dt))

        def sem(name):
            return ctx.enter_context(nc.semaphore(name))

        words = sb("words", [P, NS, T, SUP, W1 // 2], U32)
        xs = sb("xs", [P, T, D], F32)
        arena = sb("arena", [P, 123 * KB + 256], U8)
        ident = sb("ident", [P, P], F32)
        ones = sb("ones", [P, P], F32)
        pack4 = sb("pack4", [P, W4], BF16)
        stat = sb("stat", [P, 8, T], F32)
        w_cat = sb("w_cat", [D, D + 2], F32)
        flag = sb("flag", [P, 1], I32)
        d_abs = sb("d_abs", [P, 2], F32)
        psum = ctx.enter_context(nc.psum_tensor("psum", [P, 8, 512], F32))
        waited = {e.engine: sem(f"waited_{n}") for n, e in
                  (("act", nc.scalar), ("dve", nc.vector), ("pe", nc.tensor), ("pool", nc.gpsimd))}

        def region(lo, size, dt):
            return arena[:, lo:lo + size].bitcast(dt)

        adj_in = region(0, 64 * KB, I32).rearrange("p (s n) -> p s n", s=4)
        clamped_adj = region(64 * KB, 8 * KB, FP8).rearrange("p (s t i) -> p s t i", s=2, t=HALF)
        words4 = region(72 * KB, 4 * KB, U16).rearrange("p (s t w) -> p s t w", s=4, t=HALF)
        mask0 = region(76 * KB, 16 * KB, U8).rearrange("p (s t i) -> p s t i", s=4, t=HALF)
        h_parts = region(92 * KB, 24 * KB, BF16).rearrange("p (t c d) -> p t c d", t=T, c=3)
        any4 = region(116 * KB, HALF * W4 * 2, U32).rearrange("p (t w) -> p t w", t=HALF)
        l0_sum = region(118 * KB, 6 * D * 4, F32).rearrange("p (s c d) -> p s c d", s=2, c=3)
        GB = T * 2 * 3 * DE * 2
        gparts = region(0, GB, BF16).rearrange("p (t g c d) -> p t g c d", t=T, g=2, c=3)
        s_rows = region(49 * KB, 32 * KB, F32)
        h1 = region(0, 16 * KB, F32).rearrange("p (t d) -> p t d", t=T)
        h1_scr = region(16 * KB, 16 * KB, F32).rearrange("p (t d) -> p t d", t=T)
        wh = region(81 * KB, T * DE * 4, F32).rearrange("p (t d) -> p t d", t=T)
        g_full = region(98 * KB, T * DE * 4, F32).rearrange("p (t d) -> p t d", t=T)
        h1_t = region(115 * KB, 4 * KB, F32).rearrange("p (s n) -> p s n", s=2)[0:D]
        w_src = region(119 * KB, P * 4, F32)[0:D]
        w_t = region(120 * KB, D * 4, F32)[0:D]
        a_two = region(121 * KB, 8, F32)[0:D]
        wh_sum = region(121 * KB + 64, D * 4, F32)
        wh_mean = sb("wh_mean", [P, D], F32)
        bias_b = region(122 * KB, D * 4, F32)
        edges = region(81 * KB, 16 * KB, U8).rearrange("p (s t i) -> p s t i", s=2, t=CT)
        low = region(97 * KB, 16 * KB, U8).rearrange("p (s t i) -> p s t i", s=2, t=CT)
        sign = region(113 * KB, 8 * KB, I8).rearrange("p (s t i) -> p s t i", s=2, t=CT // 2)
        sums = region(121 * KB, SUP * 2 * DE * 4, F32).rearrange("p (b g d) -> p b g d", b=SUP, g=2)
        z_all = region(0, 32 * KB, F32).rearrange("p (t i) -> p t i", t=T)
        edges1 = region(32 * KB, 8 * KB, U8).rearrange("p (t i) -> p t i", t=T)
        row_max = region(98 * KB, P * 4, F32)
        m_diag = region(99 * KB, P * 4, F32)
        m_cols = region(100 * KB, 4 * 4, F32)
        out1 = region(101 * KB, DE * 4, F32)

        mean, inv, var, s_col, d_col, alpha, beta, tmp = (stat[:, k, :] for k in range(8))

        def over_d(v):
            return v.unsqueeze(2).broadcast_to([P, T, D])

        x_rows = x.rearrange("(t q) d -> q t d", q=P)
        out_rows = out.rearrange("(s b q) d -> s q b d", q=P, b=SUP)
        adj_rows = adj.rearrange("(b q) j -> b q j", q=P)

        def wait_apart(eng, s, value):
            eng.wait_ge(s, value)
            eng.sem_inc(waited[eng.engine], 1)

        class Chain:

            def __init__(self, eng, s):
                self.eng, self.sem, self.n = eng, s, 0

            def link(self, ins):
                ins.then_inc(self.sem, 1)
                self.n = self.n + 1
                self.eng.wait_ge(self.sem, self.n)

        def relu_layernorm(dve, chain, src, dst, scr, var_ready, dev_ready, n):
            link = chain.link
            link(nc.vector.tensor_reduce(out=mean, in_=src, axis=AXX, op=ALU.add))
            link(nc.vector.tensor_scalar(mean, mean, 1.0 / D, None, ALU.mult))
            link(nc.vector.tensor_tensor(dst, src, over_d(mean), ALU.subtract))
            link(nc.vector.tensor_tensor(scr, dst, dst, ALU.mult))
            link(nc.vector.tensor_reduce(out=var, in_=scr, axis=AXX, op=ALU.add))
            nc.vector.tensor_scalar(var, var, 1.0 / D, EPS, ALU.mult, ALU.add).then_inc(var_ready, 1)
            dve.wait_ge(dev_ready, n)
            link(nc.vector.reciprocal(inv, inv))
            link(nc.vector.tensor_tensor(tmp, inv, inv, ALU.mult))
            link(nc.vector.tensor_tensor(tmp, tmp, var, ALU.mult))
            link(nc.vector.tensor_scalar(tmp, tmp, -0.5, 1.5, ALU.mult, ALU.add))
            link(nc.vector.tensor_tensor(inv, inv, tmp, ALU.mult))
            link(nc.vector.tensor_tensor(dst, dst, over_d(inv), ALU.mult))
            link(nc.vector.tensor_scalar(dst, dst, 0.0, None, ALU.max))

        x_in = sem("x_in")
        adj_landed = [sem(f"adj_landed{k}") for k in range(4)]
        clamped, packed, evacuated = sem("clamped"), sem("packed"), sem("evacuated")
        unpacked, multiplied = sem("unpacked"), sem("multiplied")
        sum_copied, sum_added = sem("sum_copied"), sem("sum_added")
        consts_ready, v_chain, p_chain = sem("consts_ready"), sem("v_chain"), sem("p_chain")
        var_ready, dev_ready, h_ready = sem("var_ready"), sem("dev_ready"), sem("h_ready")
        NB = 4
        TURNS = T // NB
        h0 = region(76 * KB, 16 * KB, F32).rearrange("p (t d) -> p t d", t=T)
        h0_scr = words[:, 0:NS // 4, :, :, :].rearrange("p s t b w -> p (s t b w)").bitcast(F32).rearrange(
            "p (t d) -> p t d", t=T)

        def turns(eng, body):
            with eng.Fori(0, TURNS - 1) as turn:
                body(turn, False)
            body(TURNS - 1, True)

        with nc.Block() as block:
            @block.sync
            def _(sp):
                sp.dma_start(xs[:, :, :], x_rows).then_inc(x_in, 16)

                def body(turn, last):
                    for r in range(2 * NB):
                        sp.wait_ge(clamped, done(turn * (2 * NB) + r + 1 - 4))
                        sp.dma_start(adj_in[:, r % 4, :],
                                     adj_rows[turn * NB + r // 2, :, (r % 2) * (N // 2):(r % 2 + 1) * (N // 2)]
                                     ).then_inc(adj_landed[r % 4], 16)
                turns(sp, body)

            @block.vector
            def _(dve):
                dve.sem_inc(clamped, HEAD)
                dve.sem_inc(unpacked, HEAD)
                chain = Chain(dve, v_chain)
                link = chain.link
                dve.wait_ge(x_in, 16)
                relu_layernorm(dve, chain, xs[:, :, :], h0, h0_scr, var_ready, dev_ready, 1)
                link(nc.vector.tensor_copy(h_parts[:, :, 0, :], h0))
                link(nc.vector.tensor_tensor(h0_scr, h0, h_parts[:, :, 0, :], ALU.subtract))
                link(nc.vector.tensor_copy(h_parts[:, :, 1, :], h0_scr))
                nc.vector.tensor_tensor(h_parts[:, :, 2, :], h0_scr, h_parts[:, :, 1, :], ALU.subtract)
                link(nc.vector.tensor_tensor(xs[:, :, :], xs[:, :, :], h0, ALU.add))
                dve.sem_inc(h_ready, 1)

                def clamp(turn, r):
                    n = turn * (2 * NB) + r
                    landed = (turn * 2 + (r // 4 + 1)) * 16
                    dve.wait_ge(adj_landed[r % 4], landed)
                    wait_apart(dve, packed, done(n + 1 - 2))
                    nc.vector.tensor_scalar(
                        clamped_adj[:, r % 2, :, :].rearrange("p t i -> p (t i)"), adj_in[:, r % 4, :],
                        0.0, 2.0, ALU.max, ALU.min, saturate=False).then_inc(clamped, 1)

                def unpack(turn, r):
                    n = turn * (2 * NB) + r
                    dve.wait_ge(evacuated, done(n + 1))
                    dve.wait_ge(multiplied, done(n + 1 - 4))
                    dve.wait_ge(v_chain, chain.n)
                    w32 = words4[:, r % 4, :, :].rearrange("p t w -> p (t w)").bitcast(U32)
                    m16 = mask0[:, r % 4, :, :].rearrange("p t i -> p (t i)").bitcast(U16).rearrange(
                        "p (t k w) -> p t k w", t=HALF, k=4)
                    nc.vector.scalar_tensor_tensor(
                        out=any4[:, :, :].rearrange("p t w -> p (t w)"), in0=w32, scalar=1, in1=w32,
                        op0=ALU.logical_shift_right, op1=ALU.bitwise_or).then_inc(v_chain, 1)
                    for k in range(4):
                        last = nc.vector.tensor_scalar(
                            m16[:, :, k, :], words4[:, r % 4, :, :], 6 - 2 * k, 0x4040,
                            ALU.logical_shift_left, ALU.bitwise_and)
                    last.then_inc(unpacked, 1)
                    chain.n = chain.n + 1
                    dve.wait_ge(v_chain, chain.n)
                    link(nc.vector.tensor_scalar(any4[:, :, :], any4[:, :, :], 0x55555555, None, ALU.bitwise_and))
                    hs = slice((r % 2) * HALF, (r % 2 + 1) * HALF)
                    nc.vector.scalar_tensor_tensor(
                        out=words[:, turn, hs, r // 2, :],
                        in0=any4[:, :, W1 // 2:W1], scalar=1, in1=any4[:, :, 0:W1 // 2],
                        op0=ALU.logical_shift_left, op1=ALU.bitwise_or).then_inc(v_chain, 1)
                    chain.n = chain.n + 1

                clamp(0, 0)
                start = chain.n

                def body(turn, last):
                    chain.n = turn * (3 * 2 * NB) + start
                    for r in range(2 * NB):
                        if r < 2 * NB - 1:
                            clamp(turn, r + 1)
                        elif not last:
                            clamp(turn + 1, 0)
                        unpack(turn, r)
                turns(dve, body)

            @block.tensor
            def _(pe):
                pe.wait_ge(consts_ready, 1)
                pe.sem_inc(packed, HEAD)
                pe.sem_inc(multiplied, HEAD)

                def pack(turn, r):
                    n = turn * (2 * NB) + r
                    pe.wait_ge(clamped, done(n + 1))
                    wait_apart(pe, evacuated, done(n + 1 - 4))
                    for t in range(HALF):
                        last = nc.tensor.matmul(psum[:, r % 4, t * W4:(t + 1) * W4],
                                                clamped_adj[:, r % 2, t, :], pack4[:, :], start=True, stop=True)
                    last.then_inc(packed, 1)

                def multiply(turn, r):
                    n = turn * (2 * NB) + r
                    bank = 4 + (r // 2) % 2
                    if r % 2 == 0:
                        pe.wait_ge(sum_copied, done(turn * NB + r // 2 + 1 - 2))
                    wait_apart(pe, unpacked, done(n + 1))
                    m8 = mask0[:, r % 4, :, :].bitcast(FP8)
                    for t in range(HALF):
                        tt = (r % 2) * HALF + t
                        last = nc.tensor.matmul(psum[:, bank, 0:3 * D], m8[:, t, :],
                                                h_parts[:, tt, :, :].rearrange("p c d -> p (c d)"),
                                                start=(tt == 0), stop=(tt == T - 1))
                    last.then_inc(multiplied, 1)

                pack(0, 0)
                pe.wait_ge(h_ready, 1)

                def body(turn, last):
                    for r in range(2 * NB):
                        if r < 2 * NB - 1:
                            pack(turn, r + 1)
                        elif not last:
                            pack(turn + 1, 0)
                        multiply(turn, r)
                turns(pe, body)

            @block.scalar
            def _(act):
                act.sem_inc(evacuated, HEAD)
                act.sem_inc(sum_copied, HEAD)
                act.wait_ge(var_ready, 1)
                nc.scalar.activation(inv, var, ACT.Sqrt).then_inc(dev_ready, 1)

                def evacuate(turn, r):
                    n = turn * (2 * NB) + r
                    act.wait_ge(packed, done(n + 1))
                    act.wait_ge(unpacked, done(n + 1 - 4))
                    nc.scalar.activation(words4[:, r % 4, :, :].rearrange("p t w -> p (t w)"),
                                         psum[:, r % 4, :], ACT.Copy).then_inc(evacuated, 1)

                def copy_sum(turn, r):
                    b = turn * NB + r // 2
                    act.wait_ge(multiplied, done(turn * (2 * NB) + r + 1))
                    act.wait_ge(sum_added, done(b + 1 - 2))
                    nc.scalar.activation(l0_sum[:, (r // 2) % 2, :, :].rearrange("p c d -> p (c d)"),
                                         psum[:, 4 + (r // 2) % 2, 0:3 * D], ACT.Copy, scale=0.5
                                         ).then_inc(sum_copied, 1)

                evacuate(0, 0)

                def body(turn, last):
                    for r in range(2 * NB):
                        if r < 2 * NB - 1:
                            evacuate(turn, r + 1)
                        elif not last:
                            evacuate(turn + 1, 0)
                        if r % 2 == 1:
                            copy_sum(turn, r)
                turns(act, body)

            @block.gpsimd
            def _(pool):
                chain = Chain(pool, p_chain)
                link = chain.link
                pool.sem_inc(sum_added, HEAD)
                link(nc.gpsimd.memset(pack4[:, :], 0.0))
                for k in range(4):
                    for e in range(2):
                        link(nc.gpsimd.affine_select(
                            out=pack4[:, :], in_=pack4[:, :], compare_op=ALU.not_equal,
                            fill=float(4 ** (k + 4 * e)), base=-(32 * k + e), pattern=[[-2, W4]],
                            channel_multiplier=1))
                pool.sem_inc(consts_ready, 1)
                nc.gpsimd.memset(ones[:, :], 1.0)
                link(nc.gpsimd.memset(ident[:, :], 0.0))
                link(nc.gpsimd.affine_select(out=ident[:, :], in_=ident[:, :], compare_op=ALU.not_equal,
                                             fill=1.0, base=0, pattern=[[-1, P]], channel_multiplier=1))
                pool.wait_ge(h_ready, 1)
                start = chain.n

                def body(turn, last):
                    chain.n = turn * (2 * NB) + start
                    for r in range(NB):
                        pool.wait_ge(sum_copied, done(turn * NB + r + 1))
                        a = l0_sum[:, r % 2, :, :]
                        link(nc.gpsimd.tensor_tensor(a[:, 1, :], a[:, 1, :], a[:, 2, :], ALU.add))
                        link(nc.gpsimd.tensor_tensor(a[:, 0, :], a[:, 0, :], a[:, 1, :], ALU.add))
                        xb = xs[:, turn * NB + r, :]
                        nc.gpsimd.tensor_tensor(xb, xb, a[:, 0, :], ALU.add).then_inc(sum_added, 1)
                turns(pool, body)

        w_in, wt_ready, wt_copied = sem("w_in"), sem("wt_ready"), sem("wt_copied")
        wa_ready, w_cat_ready = sem("wa_ready"), sem("w_cat_ready")
        h1_ready, turned, h1_t_ready = sem("h1_ready"), sem("turned"), sem("h1_t_ready")
        projected, s_copied, wh_copied = sem("projected"), sem("s_copied"), sem("wh_copied")
        mid_v, mid_p = sem("mid_v"), sem("mid_p")
        var1_ready, dev1_ready = sem("var1_ready"), sem("dev1_ready")
        exp_ready, e_used, mean_sum_ready, mean_ready = (
            sem("exp_ready"), sem("e_used"), sem("mean_sum_ready"), sem("mean_ready"))
        d_abs_ready, d_all_ready = sem("d_abs_ready"), sem("d_all_ready")

        with nc.Block() as block:
            @block.sync
            def _(sp):
                sp.dma_start(w_cat[:, 0:D], weight_w).then_inc(w_in, 16)
                with nc.allow_non_contiguous_dma(reason="128 numbers"):
                    sp.dma_start(a_two, weight_a.rearrange("(k o) c -> o (k c)", k=2)).then_inc(w_in, 16)
                sp.dma_start(bias_b, bias.rearrange("(a d) -> a d", a=1).broadcast_to([P, D])).then_inc(w_in, 16)

            @block.tensor
            def _(pe):
                pe.wait_ge(w_in, 48)
                nc.tensor.transpose(psum[0:D, 6, 0:D], w_cat[:, 0:D], ident[0:D, 0:D]).then_inc(wt_ready, 1)
                pe.wait_ge(wt_copied, 1)
                nc.tensor.matmul(psum[0:D, 7, 0:2], w_t, a_two, start=True, stop=True).then_inc(wa_ready, 1)
                pe.wait_ge(w_cat_ready, 1)
                pe.wait_ge(h1_ready, 1)

                def turn_block(g):
                    if g >= 2:
                        pe.wait_ge(h1_t_ready, g - 1)
                    for k in range(SUP):
                        last = nc.tensor.transpose(psum[0:D, g % 2, k * P:(k + 1) * P],
                                                   h1[:, g * SUP + k, :], ident[:, :])
                    last.then_inc(turned, 1)

                turn_block(0)
                for g in range(NS):
                    if g + 1 < NS:
                        turn_block(g + 1)
                    pe.wait_ge(h1_t_ready, g + 1)
                    if g >= 2:
                        pe.wait_ge(s_copied, g - 1)
                        pe.wait_ge(wh_copied, g - 1)
                    nc.tensor.matmul(psum[:, 2 + g % 2, :], w_src, h1_t[:, g % 2, :], start=True, stop=True)
                    for k in range(SUP):
                        last = nc.tensor.matmul(psum[:, 4 + g % 2, k * (D + 2):(k + 1) * (D + 2)],
                                                h1_t[:, g % 2, k * P:(k + 1) * P], w_cat[:, :],
                                                start=True, stop=True)
                    last.then_inc(projected, 1)
                pe.wait_ge(mean_sum_ready, 1)
                nc.tensor.matmul(psum[:, 6, 0:D], ones[:, :], wh_sum, start=True, stop=True).then_inc(mean_ready, 1)

            @block.scalar
            def _(act):
                act.wait_ge(var1_ready, 1)
                nc.scalar.activation(inv, var, ACT.Sqrt).then_inc(dev1_ready, 1)
                for g in range(NS):
                    act.wait_ge(turned, g + 1)
                    if g >= 2:
                        act.wait_ge(projected, g - 1)
                    nc.scalar.activation(h1_t[:, g % 2, :], psum[0:D, g % 2, :], ACT.Copy).then_inc(h1_t_ready, 1)
                    if g >= 1:
                        act.wait_ge(projected, g)
                        nc.scalar.activation(s_rows[:, (g - 1) * SUPW:g * SUPW], psum[:, 2 + (g - 1) % 2, :],
                                             ACT.Copy).then_inc(s_copied, 1)
                act.wait_ge(projected, NS)
                nc.scalar.activation(s_rows[:, (NS - 1) * SUPW:], psum[:, 2 + (NS - 1) % 2, :],
                                     ACT.Copy).then_inc(s_copied, 1)
                act.wait_ge(wh_copied, NS)
                nc.scalar.activation(mean, d_col, ACT.Exp)
                nc.scalar.activation(var, d_col, ACT.Exp, scale=SLOPE)
                nc.scalar.activation(alpha, s_col, ACT.Exp, scale=1.0 - SLOPE)
                nc.scalar.activation(beta, s_col, ACT.Exp, scale=SLOPE - 1.0).then_inc(exp_ready, 1)

            @block.vector
            def _(dve):
                chain = Chain(dve, mid_v)
                link = chain.link
                dve.wait_ge(wt_ready, 1)
                nc.vector.tensor_copy(w_t, psum[0:D, 6, 0:D]).then_inc(wt_copied, 1)
                dve.wait_ge(wa_ready, 1)
                link(nc.vector.tensor_copy(w_cat[:, D:D + 2], psum[0:D, 7, 0:2]))
                nc.vector.tensor_scalar(w_src, ones[0:D, :], w_cat[:, D:D + 1], None, ALU.mult).then_inc(w_cat_ready, 1)
                relu_layernorm(dve, chain, xs[:, :, :], h1, h1_scr, var1_ready, dev1_ready, 1)
                dve.sem_inc(h1_ready, 1)
                dve.wait_ge(w_in, 48)
                nc.vector.tensor_tensor(xs[:, :, :], xs[:, :, :], bias_b.unsqueeze(1).broadcast_to([P, T, D]),
                                        ALU.add)
                nc.vector.memset(wh[:, :, D:DE], 1.0)
                for g in range(NS):
                    dve.wait_ge(projected, g + 1)
                    got = psum[:, 4 + g % 2, 0:SUP * (D + 2)].rearrange("p (k n) -> p k n", k=SUP)
                    ts = slice(g * SUP, (g + 1) * SUP)
                    nc.vector.tensor_copy(wh[:, ts, 0:D], got[:, :, 0:D])
                    nc.vector.tensor_copy(s_col[:, ts], got[:, :, D])
                    nc.vector.tensor_copy(d_col[:, ts], got[:, :, D + 1]).then_inc(wh_copied, 1)
                dve.wait_ge(wh_copied, NS)
                link(nc.vector.tensor_reduce(out=d_abs[:, 0:1], in_=d_col, axis=AXX, op=ALU.max,
                                             apply_absolute_value=True))
                dve.sem_inc(d_abs_ready, 1)
                link(nc.vector.tensor_reduce(out=wh_sum, in_=wh[:, :, 0:D].rearrange("p t d -> p d t"),
                                             axis=AXX, op=ALU.add))
                dve.sem_inc(mean_sum_ready, 1)
                dve.wait_ge(exp_ready, 1)
                nc.vector.tensor_scalar(alpha, alpha, 1.0, None, ALU.min)
                nc.vector.tensor_scalar(beta, beta, 1.0, None, ALU.min)
                dve.wait_ge(s_copied, NS)
                for g, e in enumerate((mean, var)):
                    link(nc.vector.tensor_tensor(g_full, wh, e.unsqueeze(2).broadcast_to([P, T, DE]), ALU.mult))
                    link(nc.vector.tensor_copy(gparts[:, :, g, 0, :], g_full))
                    link(nc.vector.tensor_tensor(g_full, g_full, gparts[:, :, g, 0, :], ALU.subtract))
                    link(nc.vector.tensor_copy(gparts[:, :, g, 1, :], g_full))
                    link(nc.vector.tensor_tensor(gparts[:, :, g, 2, :], g_full, gparts[:, :, g, 1, :], ALU.subtract))
                dve.wait_ge(mean_ready, 1)
                nc.vector.tensor_scalar(wh_mean[:, :], psum[:, 6, 0:D], 1.0 / N, None, ALU.mult)
                dve.wait_ge(d_all_ready, 1)
                nc.vector.tensor_scalar(flag[:, :], d_abs[:, 1:2], SAFE, None, ALU.is_gt)

            @block.gpsimd
            def _(pool):
                pool.wait_ge(d_abs_ready, 1)
                nc.gpsimd.partition_all_reduce(d_abs[:, 1:2], d_abs[:, 0:1], P, RMAX).then_inc(d_all_ready, 1)

        signs_ready, low_ready, masks_ready = sem("signs_ready"), sem("low_ready"), sem("masks_ready")
        chunk_done, first_copied, sums_ready = sem("chunk_done"), sem("first_copied"), sem("sums_ready")
        rows_out, out_done, l1_v, l1_p = sem("rows_out"), sem("out_done"), sem("l1_v"), sem("l1_p")
        den_ready, rec_ready = sem("den_ready"), sem("rec_ready")
        gen_v, gen_turned, gen_mdiag, gen_m = sem("gen_v"), sem("gen_turned"), sem("gen_mdiag"), sem("gen_m")
        gen_max, gen_z, gen_exp, gen_e, gen_sum = (
            sem("gen_max"), sem("gen_z"), sem("gen_exp"), sem("gen_e"), sem("gen_sum"))
        gen_rows = sem("gen_rows")
        HC = CT // 2
        fin = sb("fin", [P, SUP, 3], F32)

        with nc.Block() as block:
            @block.sync
            def _(sp):
                general = sp.value_load(flag[0:1, 0:1], min_val=0, max_val=1)
                with sp.If(general == 0):
                    with sp.Fori(0, NS) as s:
                        sp.wait_ge(rows_out, s + 1)
                        sp.dma_start(out_rows[s], xs[:, bass.ds(s * SUP, SUP), :]).then_inc(out_done, 16)
                with sp.Else():
                    with sp.Fori(0, NS) as s:
                        sp.wait_ge(gen_rows, s * SUP + SUP)
                        sp.dma_start(out_rows[s], xs[:, bass.ds(s * SUP, SUP), :]).then_inc(out_done, 16)
                sp.wait_ge(out_done, 16 * NS)

            @block.scalar
            def _(act):
                general = act.value_load(flag[0:1, 0:1], min_val=0, max_val=1)
                with act.If(general == 0):
                    act.sem_inc(signs_ready, HEAD)
                    act.sem_inc(first_copied, HEAD)

                    def signs(s, h):
                        u = s * (2 * NCH) + h
                        wait_apart(act, low_ready, done(u + 1 - 2))
                        for k in range(HC):
                            t = h * HC + k
                            last = nc.scalar.activation(sign[:, h % 2, k, :], s_rows[:, bass.ds(s * SUPW, SUPW)],
                                                        ACT.Sign, bias=d_col[:, t:t + 1])
                        last.then_inc(signs_ready, 1)

                    def copy_first(s, par):
                        act.wait_ge(chunk_done, done(s * NCH + NCH))
                        act.wait_ge(rows_out, s)
                        src = psum[:, 4 * par:4 * par + SUP, 0:6 * DE].rearrange("p b (g c d) -> p b g c d", g=2, c=3)
                        for g in range(2):
                            last = nc.scalar.activation(sums[:, :, g, :], src[:, :, g, 0, :], ACT.Copy)
                        last.then_inc(first_copied, 1)

                    for h in range(4):
                        signs(0, h)
                    with act.Fori(0, NS // 2 - 1) as pair:
                        for par in range(2):
                            s = pair * 2 + par
                            for h in range(4, 2 * NCH):
                                signs(s, h)
                            for h in range(4):
                                signs(s + 1, h)
                            copy_first(s, par)
                    for par in range(2):
                        s = NS - 2 + par
                        for h in range(4, 2 * NCH):
                            signs(s, h)
                        if par == 0:
                            for h in range(4):
                                signs(s + 1, h)
                        copy_first(s, par)
                with act.Else():
                    with act.Fori(0, T) as b:
                        act.wait_ge(gen_z, b + 1)
                        nc.scalar.activation(z_all, z_all, ACT.Exp).then_inc(gen_exp, 1)

            @block.vector
            def _(dve):
                general = dve.value_load(flag[0:1, 0:1], min_val=0, max_val=1)
                with dve.If(general == 0):
                    dve.sem_inc(low_ready, HEAD)
                    dve.sem_inc(masks_ready, HEAD)

                    def chunk(s, c):
                        v = s * NCH + c
                        slot = c % 2
                        dve.wait_ge(chunk_done, done(v + 1 - 2))
                        w16 = words[:, s, c * CT:(c + 1) * CT, :, :].rearrange("p t b w -> p (t b w)").bitcast(
                            U16).rearrange("p (n w) -> p n w", w=W1)
                        e16 = edges[:, slot, :, :].rearrange("p t i -> p (t i)").bitcast(U16)
                        l16 = low[:, slot, :, :].rearrange("p t i -> p (t i)").bitcast(U16)
                        e_view = e16.rearrange("p (n m w) -> p n m w", m=8, w=W1)
                        for m in range(8):
                            op, by = (ALU.logical_shift_left, 6 - m) if m <= 6 else (ALU.logical_shift_right, 1)
                            last = nc.vector.tensor_scalar(e_view[:, :, m, :], w16, by, 0x4040, op, ALU.bitwise_and)
                        last.then_inc(l1_v, 1)
                        dve.wait_ge(l1_v, v + 1)
                        n2 = HC * SUPW // 2
                        for k in range(2):
                            h = 2 * c + k
                            u = s * (2 * NCH) + h
                            dve.wait_ge(signs_ready, done(u + 1))
                            part = slice(k * n2, (k + 1) * n2)
                            g16 = sign[:, h % 2, :, :].rearrange("p t i -> p (t i)").bitcast(U16)
                            nc.vector.tensor_tensor(l16[:, part], e16[:, part], g16, ALU.bitwise_and
                                                    ).then_inc(low_ready, 1)
                        for k in range(2):
                            u = s * (2 * NCH) + 2 * c + k
                            part = slice(k * n2, (k + 1) * n2)
                            dve.wait_ge(low_ready, done(u + 1))
                            nc.vector.tensor_tensor(e16[:, part], e16[:, part], l16[:, part], ALU.bitwise_xor
                                                    ).then_inc(masks_ready, 1)

                    def add_parts(s, par):
                        src = psum[:, 4 * par:4 * par + SUP, 0:6 * DE].rearrange("p b (g c d) -> p b g c d", g=2, c=3)
                        dve.wait_ge(first_copied, done(s + 1))
                        for g in range(2):
                            last = nc.vector.tensor_tensor(sums[:, :, g, :], sums[:, :, g, :], src[:, :, g, 1, :], ALU.add)
                        last.then_inc(sums_ready, 1)
                        dve.wait_ge(sums_ready, s * 2 + 1)
                        for g in range(2):
                            last = nc.vector.tensor_tensor(sums[:, :, g, :], sums[:, :, g, :], src[:, :, g, 2, :], ALU.add)
                        last.then_inc(sums_ready, 1)

                    def invert(s):
                        dve.wait_ge(den_ready, s + 1)
                        nc.vector.reciprocal(fin[:, :, 2], fin[:, :, 1]).then_inc(rec_ready, 1)

                    chunk(0, 0)
                    chunk(0, 1)
                    with dve.Fori(0, NS // 2 - 1) as pair:
                        for par in range(2):
                            s = pair * 2 + par
                            for c in range(2, NCH):
                                chunk(s, c)
                            chunk(s + 1, 0)
                            chunk(s + 1, 1)
                            add_parts(s, par)
                            invert(s)
                    for par in range(2):
                        s = NS - 2 + par
                        for c in range(2, NCH):
                            chunk(s, c)
                        if par == 0:
                            chunk(s + 1, 0)
                            chunk(s + 1, 1)
                        add_parts(s, par)
                        invert(s)
                with dve.Else():
                    STEPS = 19
                    w_view = words[:, :, :, :, :]
                    with dve.Fori(0, NS) as s:
                        for k in range(SUP):
                            b = s * SUP + k
                            count = [0]

                            def link(ins):
                                count[0] += 1
                                ins.then_inc(gen_v, 1)
                                wait_apart(dve, gen_v, b * STEPS + count[0])

                            e16 = edges1.rearrange("p t i -> p (t i)").bitcast(U16).rearrange(
                                "p (n m w) -> p n m w", m=8, w=W1)
                            w16 = w_view[:, s, :, k, :].bitcast(U16)
                            if True:
                                dve.wait_ge(gen_rows, b)
                            for m in range(8):
                                op, by = (ALU.logical_shift_left, 6 - m) if m <= 6 else (ALU.logical_shift_right, 1)
                                last = nc.vector.tensor_scalar(e16[:, :, m, :], w16, by, 0x4040, op, ALU.bitwise_and)
                            link(last)
                            e8 = edges1.bitcast(FP8)
                            link(nc.vector.tensor_scalar(tmp, d_col, d_abs[:, 1:2], None, ALU.add))
                            link(nc.vector.tensor_tensor(z_all, e8, tmp.unsqueeze(2).broadcast_to([P, T, P]), ALU.mult))
                            link(nc.vector.tensor_reduce(out=row_max, in_=z_all.rearrange("p t i -> p i t"),
                                                         axis=AXX, op=ALU.max))
                            dve.sem_inc(gen_max, 1)
                            dve.wait_ge(gen_turned, b + 1)
                            link(nc.vector.tensor_reduce(out=m_cols[:, 0:1], in_=psum[:, 0, 0:P], axis=AXX, op=ALU.max))
                            link(nc.vector.tensor_scalar(m_cols[:, 0:1], m_cols[:, 0:1], 0.5, d_abs[:, 1:2],
                                                         ALU.mult, ALU.subtract))
                            link(nc.vector.tensor_tensor(m_cols[:, 0:1], m_cols[:, 0:1], s_col[:, bass.ds(b, 1)], ALU.add))
                            link(nc.vector.scalar_tensor_tensor(out=m_cols[:, 1:2], in0=m_cols[:, 0:1], scalar=SLOPE,
                                                                in1=m_cols[:, 0:1], op0=ALU.mult, op1=ALU.max))
                            link(nc.vector.tensor_scalar(m_diag, ident[:, :], m_cols[:, 1:2], None, ALU.mult))
                            dve.sem_inc(gen_mdiag, 1)
                            link(nc.vector.tensor_tensor(
                                z_all, s_rows[:, bass.ds(b * P, P)].unsqueeze(1).broadcast_to([P, T, P]),
                                d_col.unsqueeze(2).broadcast_to([P, T, P]), ALU.add))
                            link(nc.vector.scalar_tensor_tensor(out=z_all, in0=z_all, scalar=SLOPE, in1=z_all,
                                                                op0=ALU.mult, op1=ALU.max))
                            dve.wait_ge(gen_m, b + 1)
                            link(nc.vector.tensor_tensor(
                                z_all, z_all, psum[:, 1, 0:P].unsqueeze(1).broadcast_to([P, T, P]), ALU.subtract))
                            link(nc.vector.tensor_scalar(z_all, z_all, 0.0, None, ALU.min))
                            dve.sem_inc(gen_z, 1)
                            wait_apart(dve, gen_exp, b + 1)
                            link(nc.vector.tensor_tensor(z_all, z_all, e8, ALU.mult))
                            dve.sem_inc(gen_e, 1)
                            dve.wait_ge(gen_sum, b + 1)
                            link(nc.vector.tensor_copy(out1, psum[:, 2, 0:DE]))
                            link(nc.vector.tensor_scalar(m_cols[:, 2:3], out1[:, D:DE], 0.0, None, ALU.is_equal))
                            link(nc.vector.scalar_tensor_tensor(out=out1[:, 0:D], in0=wh_mean[:, :], scalar=m_cols[:, 2:3],
                                                                in1=out1[:, 0:D], op0=ALU.mult, op1=ALU.add))
                            link(nc.vector.tensor_tensor(out1[:, D:DE], out1[:, D:DE], m_cols[:, 2:3], ALU.add))
                            link(nc.vector.reciprocal(m_cols[:, 3:4], out1[:, D:DE]))
                            xb = xs[:, b, :]
                            nc.vector.scalar_tensor_tensor(out=xb, in0=out1[:, 0:D], scalar=m_cols[:, 3:4], in1=xb,
                                                           op0=ALU.mult, op1=ALU.add).then_inc(gen_rows, 1)
                            assert count[0] == STEPS

            @block.tensor
            def _(pe):
                general = pe.value_load(flag[0:1, 0:1], min_val=0, max_val=1)
                with pe.If(general == 0):
                    pe.sem_inc(chunk_done, HEAD)
                    with pe.Fori(0, NS // 2) as pair:
                        for par in range(2):
                            s = pair * 2 + par
                            pe.wait_ge(first_copied, done(s + 1 - 2))
                            for c in range(NCH):
                                v = s * NCH + c
                                for t in range(CT):
                                    if t % HC == 0:
                                        wait_apart(pe, masks_ready, done(v * 2 + t // HC + 1))
                                    tt = c * CT + t
                                    for b in range(SUP):
                                        for g, m in ((0, edges), (1, low)):
                                            last = nc.tensor.matmul(
                                                psum[:, 4 * par + b, g * 3 * DE:(g + 1) * 3 * DE],
                                                m[:, c % 2, t, b * P:(b + 1) * P].bitcast(FP8),
                                                gparts[:, tt, g, :, :].rearrange("p c d -> p (c d)"),
                                                start=(tt == 0 and g == 0), stop=(tt == T - 1),
                                                skip_group_check=True)
                                last.then_inc(chunk_done, 1)
                with pe.Else():
                    with pe.Fori(0, T) as b:
                        pe.wait_ge(gen_max, b + 1)
                        nc.tensor.transpose(psum[:, 0, 0:P], row_max, ident[:, :]).then_inc(gen_turned, 1)
                        pe.wait_ge(gen_mdiag, b + 1)
                        nc.tensor.matmul(psum[:, 1, 0:P], ones[:, :], m_diag, start=True, stop=True).then_inc(gen_m, 1)
                        pe.wait_ge(gen_e, b + 1)
                        for t in range(T):
                            last = nc.tensor.matmul(psum[:, 2, 0:DE], z_all[:, t, :], wh[:, t, :],
                                                    start=(t == 0), stop=(t == T - 1))
                        last.then_inc(gen_sum, 1)

            @block.gpsimd
            def _(pool):
                general = pool.value_load(flag[0:1, 0:1], min_val=0, max_val=1)
                with pool.If(general == 0):
                    STEPS = 7
                    with pool.Fori(0, NS) as s:
                        count = [0]

                        def link(ins):
                            count[0] += 1
                            ins.then_inc(l1_p, 1)
                            wait_apart(pool, l1_p, s * STEPS + count[0])

                        pool.wait_ge(sums_ready, s * 2 + 2)
                        for g, f in ((0, alpha), (1, beta)):
                            last = nc.gpsimd.tensor_tensor(
                                sums[:, :, g, :], sums[:, :, g, :],
                                f[:, bass.ds(s * SUP, SUP)].unsqueeze(2).broadcast_to([P, SUP, DE]), ALU.mult)
                        link(last)
                        num = sums[:, :, 0, :]
                        link(nc.gpsimd.tensor_tensor(num, num, sums[:, :, 1, :], ALU.add))
                        link(nc.gpsimd.tensor_scalar(fin[:, :, 0], num[:, :, D], 0.0, None, ALU.is_equal))
                        link(nc.gpsimd.tensor_tensor(fin[:, :, 1], num[:, :, D], fin[:, :, 0], ALU.add))
                        pool.sem_inc(den_ready, 1)
                        link(nc.gpsimd.tensor_tensor(
                            sums[:, :, 1, 0:D], wh_mean[:, :].unsqueeze(1).broadcast_to([P, SUP, D]),
                            fin[:, :, 0].unsqueeze(2).broadcast_to([P, SUP, D]), ALU.mult))
                        link(nc.gpsimd.tensor_tensor(num[:, :, 0:D], num[:, :, 0:D], sums[:, :, 1, 0:D], ALU.add))
                        pool.wait_ge(rec_ready, s + 1)
                        link(nc.gpsimd.tensor_tensor(num[:, :, 0:D], num[:, :, 0:D],
                                                     fin[:, :, 2].unsqueeze(2).broadcast_to([P, SUP, D]), ALU.mult))
                        xb = xs[:, bass.ds(s * SUP, SUP), :]
                        nc.gpsimd.tensor_tensor(xb, xb, num[:, :, 0:D], ALU.add).then_inc(rows_out, 1)
                        assert count[0] == STEPS


def kernel(x, adj, L1_gnn_weight_w, L1_gnn_weight_a, L1_gnn_bias):
    import numpy as np
    import concourse.bacc as bacc
    from concourse.bass_utils import run_bass_kernel_spmd

    nc = bacc.Bacc("TRN2", target_bir_lowering=False, num_devices=1)
    arrays, args = {}, []
    for name, a in (("x", x), ("adj", adj), ("weight_w", L1_gnn_weight_w),
                    ("weight_a", L1_gnn_weight_a), ("bias", L1_gnn_bias)):
        a = np.ascontiguousarray(a)
        arrays[name] = a
        args.append(nc.dram_tensor(name, a.shape, mybir.dt.from_np(a.dtype), kind="ExternalInput").ap())
    args.append(nc.dram_tensor("out", x.shape, mybir.dt.float32, kind="ExternalOutput").ap())
    gnn_two_layers(nc, *args)
    r = run_bass_kernel_spmd(nc, [arrays], core_ids=[0])
    return r.results[0]["out"]
```

```python
import concourse.bass as bass
import concourse.mybir as mybir
from contextlib import ExitStack

F32 = mybir.dt.float32
BF16 = mybir.dt.bfloat16
FP8 = mybir.dt.float8e4
I32 = mybir.dt.int32
I8 = mybir.dt.int8
U8 = mybir.dt.uint8
U16 = mybir.dt.uint16
U32 = mybir.dt.uint32
ALU = mybir.AluOpType
ACT = mybir.ActivationFunctionType
AXX = mybir.AxisListType.X
RMAX = bass.bass_isa.ReduceOp.max


def gnn_two_layers(
    nc: bass.Bass,
    x: bass.AP,
    adj: bass.AP,
    weight_w: bass.AP,
    weight_a: bass.AP,
    bias: bass.AP,
    out: bass.AP,
):
    N, D = x.shape
    P = 128
    T = N // P
    HALF = T // 2
    SUP = 4
    NS = T // SUP
    W4 = P // 8
    W1 = P // 16
    DE = D + 1
    SUPW = SUP * P
    CT = 16
    NCH = T // CT
    SAFE = 50.0
    SLOPE = 0.01
    EPS = 1e-5
    KB = 1024
    HEAD = 4

    def done(k):
        return k + HEAD

    ctx = ExitStack()
    with ctx:
        def sb(name, shape, dt):
            return ctx.enter_context(nc.sbuf_tensor(name, shape, dt))

        def sem(name):
            return ctx.enter_context(nc.semaphore(name))

        words = sb("words", [P, NS, T, SUP, W1 // 2], U32)
        g_flat = sb("gparts", [P, T * 2 * 3 * DE], BF16)
        gparts = g_flat[:, :].rearrange("p (t g c d) -> p t g c d", t=T, g=2, c=3)
        arena = sb("arena", [P, 88 * KB], U8)
        ident = sb("ident", [P, P], F32)
        ones = sb("ones", [P, P], F32)
        pack4 = sb("pack4", [P, W4], BF16)
        s_col = sb("s_col", [P, T], F32)
        d_col = sb("d_col", [P, T], F32)
        w_cat = sb("w_cat", [D, D + 2], F32)
        wh_mean = sb("wh_mean", [P, D], F32)
        bias_b = sb("bias_b", [P, D], F32)
        flag = sb("flag", [P, 1], I32)
        d_abs = sb("d_abs", [P, 2], F32)
        psum = ctx.enter_context(nc.psum_tensor("psum", [P, 8, 512], F32))
        x1_dram = nc.dram_tensor("x1_rows", [T, P, D], F32, kind="Internal").ap()
        wh_dram = nc.dram_tensor("wh_rows", [T, P, D], F32, kind="Internal").ap()
        s_dram = nc.dram_tensor("s_row", [1, N], F32, kind="Internal").ap()
        waited = {e.engine: sem(f"waited_{n}") for n, e in
                  (("act", nc.scalar), ("dve", nc.vector), ("pe", nc.tensor), ("pool", nc.gpsimd))}

        def region(lo, size, dt):
            return arena[:, lo:lo + size].bitcast(dt)

        QUART = N // 4
        adj_in = region(0, 32 * KB, I32).rearrange("p (s n) -> p s n", s=4)
        clamped_adj = region(32 * KB, 8 * KB, FP8).rearrange("p (s t i) -> p s t i", s=2, t=HALF)
        words4 = region(40 * KB, 4 * KB, U16).rearrange("p (s t w) -> p s t w", s=4, t=HALF)
        mask0 = region(44 * KB, 8 * KB, U8).rearrange("p (s t i) -> p s t i", s=2, t=HALF)
        h_parts = region(52 * KB, 24 * KB, BF16).rearrange("p (t c d) -> p t c d", t=T, c=3)
        any4 = region(76 * KB, HALF * W4 * 2, U32).rearrange("p (t w) -> p t w", t=HALF)
        l0_sum = region(77 * KB, 6 * D * 4, F32).rearrange("p (s c d) -> p s c d", s=2, c=3)
        SD = SUP * D * 4

        def super_rows(lo):
            return region(lo, SD, F32).rearrange("p (b d) -> p b d", b=SUP)

        x_sup, x1_sup = super_rows(79 * KB), super_rows(80 * KB)
        h1, square = super_rows(81 * KB), super_rows(82 * KB)
        h1_t = region(83 * KB, 2 * KB, F32)[0:D]
        wh = region(85 * KB, SUP * DE * 4, F32).rearrange("p (b d) -> p b d", b=SUP)
        wh_sum = super_rows(86 * KB + 64)
        small = region(87 * KB + 64, 8 * SUP * 4, F32).rearrange("p (k b) -> p k b", k=8)
        s_row = sb("s_row_sb", [1, SUPW], F32)
        g_full = sb("g_full", [P, 2, SUP, DE], F32)
        w_t = region(87 * KB + 256, D * 4, F32)[0:D]
        a_two = region(87 * KB + 512, 8, F32)[0:D]
        exps = region(87 * KB + 576, 2 * SUP * 4, F32).rearrange("p (g b) -> p g b", g=2)
        early = g_flat[:, :].bitcast(F32)
        HD = HALF * D
        x_all = early[:, 0:2 * HD].rearrange("p (k t d) -> p k t d", k=2, t=HALF)
        h_all = early[:, 2 * HD:4 * HD].rearrange("p (k t d) -> p k t d", k=2, t=HALF)
        sq_all = early[:, 4 * HD:5 * HD].rearrange("p (t d) -> p t d", t=HALF)
        st_all = early[:, 5 * HD:5 * HD + 4 * HALF].rearrange("p (k t) -> p k t", k=4)
        edges = region(0, 16 * KB, U8).rearrange("p (s t i) -> p s t i", s=2, t=CT)
        low = region(16 * KB, 16 * KB, U8).rearrange("p (s t i) -> p s t i", s=2, t=CT)
        sign = region(32 * KB, 8 * KB, I8).rearrange("p (s t i) -> p s t i", s=2, t=CT // 2)
        sums = region(40 * KB, SUP * 2 * DE * 4, F32).rearrange("p (b g d) -> p b g d", b=SUP, g=2)
        s_rows = region(43 * KB, 4 * KB, F32).rearrange("p (s i) -> p s i", s=2)
        x1_back = region(47 * KB, 2 * KB, F32).rearrange("p (s b d) -> p s b d", s=2, b=SUP)
        alpha = region(49 * KB, T * 4, F32)
        beta = region(49 * KB + 256, T * 4, F32)
        z_all = g_flat[:, :].bitcast(F32)[:, 0:T * P].rearrange(
            "p (t i) -> p t i", t=T)
        edges1 = region(0, 8 * KB, U8).rearrange("p (t i) -> p t i", t=T)
        wh_all = region(8 * KB, T * DE * 4, F32).rearrange("p (t d) -> p t d", t=T)
        s_rows_all = region(50 * KB, 32 * KB, F32)
        row_max = region(26 * KB, P * 4, F32)
        m_diag = region(27 * KB, P * 4, F32)
        m_cols = region(28 * KB, 4 * 4, F32)
        out1 = region(29 * KB, DE * 4, F32)
        tmp = region(30 * KB, T * 4, F32)
        x1_all = region(32 * KB, 16 * KB, F32).rearrange("p (t d) -> p t d", t=T)

        x_rows = x.rearrange("(t q) d -> q t d", q=P)
        out_rows = out.rearrange("(s b q) d -> s q b d", q=P, b=SUP)
        adj_rows = adj.rearrange("(b q) j -> b q j", q=P)
        x_sups = x.rearrange("(s b q) d -> s q b d", q=P, b=SUP)
        x1_sups = x1_dram.rearrange("(s b) q d -> s q b d", b=SUP)
        wh_sups = wh_dram.rearrange("(s b) q d -> s q b d", b=SUP)
        s_sups = s_dram.rearrange("a (s i) -> s a i", i=SUPW)

        def wait_apart(eng, s, value):
            eng.wait_ge(s, value)
            eng.sem_inc(waited[eng.engine], 1)

        class Chain:

            def __init__(self, eng, s, wait=None):
                self.eng, self.sem, self.n = eng, s, 0
                self.wait = wait or (lambda e, s, value: e.wait_ge(s, value))

            def link(self, ins):
                ins.then_inc(self.sem, 1)
                self.n = self.n + 1
                self.wait(self.eng, self.sem, self.n)

        def inverse_root(link, inv, var, t):
            link(nc.vector.reciprocal(inv, inv))
            link(nc.vector.tensor_tensor(t, inv, inv, ALU.mult))
            link(nc.vector.tensor_tensor(t, t, var, ALU.mult))
            link(nc.vector.tensor_scalar(t, t, -0.5, 1.5, ALU.mult, ALU.add))
            link(nc.vector.tensor_tensor(inv, inv, t, ALU.mult))

        x_in = [sem("x_in0"), sem("x_in1")]
        adj_landed = [sem(f"adj_landed{k}") for k in range(4)]
        clamped, packed, evacuated = sem("clamped"), sem("packed"), sem("evacuated")
        unpacked, multiplied = sem("unpacked"), sem("multiplied")
        sum_copied, sum_added = sem("sum_copied"), sem("sum_added")
        consts_ready, v_chain, p_chain = sem("consts_ready"), sem("v_chain"), sem("p_chain")
        ln_v, ln_a, h_ready = sem("ln_v"), sem("ln_a"), sem("h_ready")
        w_in, wt_ready, wt_copied = sem("w_in"), sem("wt_ready"), sem("wt_copied")
        wa_ready, w_cat_ready = sem("wa_ready"), sem("w_cat_ready")
        centred, var_ready, dev_ready, h1_ready = sem("centred"), sem("var_ready"), sem("dev_ready"), sem("h1_ready")
        turned, h1_t_ready, projected = sem("turned"), sem("h1_t_ready"), sem("projected")
        s_copied, wh_copied, exp_ready, g_built = sem("s_copied"), sem("wh_copied"), sem("exp_ready"), sem("g_built")
        x_landed, base_built = sem("x_landed"), sem("base_built")
        x1_stored, wh_stored, s_stored = sem("x1_stored"), sem("wh_stored"), sem("s_stored")
        d_abs_ready, d_all_ready, mean_sum_ready, mean_ready = (
            sem("d_abs_ready"), sem("d_all_ready"), sem("mean_sum_ready"), sem("mean_ready"))
        NB = SUP
        TURNS = T // NB

        def turns(eng, body):
            body(0)
            with eng.Fori(1, TURNS - 1) as turn:
                body(turn)
            body(TURNS - 1)

        def first(turn):
            return isinstance(turn, int) and turn == 0

        def last_turn(turn):
            return isinstance(turn, int) and turn == TURNS - 1

        with nc.Block() as block:
            @block.sync
            def _(sp):
                for k in range(2):
                    sp.dma_start(x_all[:, k], x_rows[:, k * HALF:(k + 1) * HALF, :]).then_inc(x_in[k], 16)

                def body(turn):
                    for m in range(4 * NB):
                        sp.wait_ge(clamped, done(turn * (4 * NB) + m + 1 - 4))
                        sp.dma_start(adj_in[:, m % 4, :],
                                     adj_rows[turn * NB + m // 4, :, (m % 4) * QUART:(m % 4 + 1) * QUART]
                                     ).then_inc(adj_landed[m % 4], 16)
                turns(sp, body)
                sp.wait_ge(x1_stored, 16 * NS)
                sp.wait_ge(wh_stored, 16 * NS + 16)
                sp.wait_ge(s_stored, 16 * NS + 16)

            @block.vector
            def _(dve):
                for s in (clamped, unpacked, centred, wh_copied):
                    dve.sem_inc(s, HEAD)
                chain = Chain(dve, v_chain)
                link = chain.link

                def norm_early(k):
                    dst = h_all[:, k]
                    mean, inv, var, t = (st_all[:, n, :] for n in range(4))
                    parts = h_parts[:, k * HALF:(k + 1) * HALF]

                    def over_d(v):
                        return v.unsqueeze(2).broadcast_to([P, HALF, D])
                    dve.wait_ge(x_in[k], 16)
                    link(nc.vector.tensor_reduce(out=mean, in_=x_all[:, k], axis=AXX, op=ALU.add))
                    link(nc.vector.tensor_scalar(mean, mean, 1.0 / D, None, ALU.mult))
                    nc.vector.tensor_tensor(dst, x_all[:, k], over_d(mean), ALU.subtract).then_inc(ln_v, 1)
                    dve.wait_ge(ln_a, 4 * k + 1)
                    link(nc.vector.tensor_reduce(out=var, in_=sq_all, axis=AXX, op=ALU.add))
                    nc.vector.tensor_scalar(var, var, 1.0 / D, EPS, ALU.mult, ALU.add).then_inc(ln_v, 1)
                    dve.wait_ge(ln_a, 4 * k + 2)
                    inverse_root(link, inv, var, t)
                    nc.vector.scalar_tensor_tensor(out=dst, in0=dst, scalar=0.0, in1=over_d(inv),
                                                   op0=ALU.max, op1=ALU.mult).then_inc(ln_v, 1)
                    dve.wait_ge(ln_a, 4 * k + 3)
                    nc.vector.tensor_tensor(sq_all, dst, parts[:, :, 0, :], ALU.subtract).then_inc(ln_v, 1)
                    dve.wait_ge(ln_a, 4 * k + 4)
                    nc.vector.tensor_tensor(parts[:, :, 2, :], sq_all, parts[:, :, 1, :], ALU.subtract
                                            ).then_inc(h_ready, 1)
                    dve.wait_ge(h_ready, k + 1)

                def clamp(turn, r):
                    n = turn * (2 * NB) + r
                    wait_apart(dve, packed, done(n + 1 - 2))
                    for q in range(2):
                        wait_apart(dve, adj_landed[2 * (r % 2) + q], (turn * NB + (r // 2 + 1)) * 16)
                        nc.vector.tensor_scalar(
                            clamped_adj[:, r % 2, q * HALF // 2:(q + 1) * HALF // 2, :].rearrange("p t i -> p (t i)"),
                            adj_in[:, 2 * (r % 2) + q, :],
                            0.0, 2.0, ALU.max, ALU.min, saturate=False).then_inc(clamped, 1)

                def unpack(turn, r):
                    n = turn * (2 * NB) + r
                    dve.wait_ge(evacuated, done(n + 1))
                    dve.wait_ge(multiplied, done(n + 1 - 2))
                    dve.wait_ge(v_chain, chain.n)
                    w32 = words4[:, r % 4, :, :].rearrange("p t w -> p (t w)").bitcast(U32)
                    m16 = mask0[:, r % 2, :, :].rearrange("p t i -> p (t i)").bitcast(U16).rearrange(
                        "p (t k w) -> p t k w", t=HALF, k=4)
                    nc.vector.scalar_tensor_tensor(
                        out=any4.rearrange("p t w -> p (t w)"), in0=w32, scalar=1, in1=w32,
                        op0=ALU.logical_shift_right, op1=ALU.bitwise_or).then_inc(v_chain, 1)
                    for k in range(4):
                        last = nc.vector.tensor_scalar(
                            m16[:, :, k, :], words4[:, r % 4, :, :], 6 - 2 * k, 0x4040,
                            ALU.logical_shift_left, ALU.bitwise_and)
                    last.then_inc(unpacked, 1)
                    chain.n = chain.n + 1
                    dve.wait_ge(v_chain, chain.n)
                    link(nc.vector.tensor_scalar(any4, any4, 0x55555555, None, ALU.bitwise_and))
                    hs = slice((r % 2) * HALF, (r % 2 + 1) * HALF)
                    nc.vector.scalar_tensor_tensor(
                        out=words[:, turn, hs, r // 2, :],
                        in0=any4[:, :, W1 // 2:W1], scalar=1, in1=any4[:, :, 0:W1 // 2],
                        op0=ALU.logical_shift_left, op1=ALU.bitwise_or).then_inc(v_chain, 1)
                    chain.n = chain.n + 1

                mean, inv, var, t4, d4 = (small[:, n, :] for n in range(5))

                def over_d(v):
                    return v.unsqueeze(2).broadcast_to([P, SUP, D])

                def centre(sup):
                    dve.wait_ge(sum_added, done(sup * SUP + SUP))
                    dve.wait_ge(turned, done(sup))
                    dve.wait_ge(v_chain, chain.n)
                    link(nc.vector.tensor_reduce(out=mean, in_=x1_sup, axis=AXX, op=ALU.add))
                    link(nc.vector.tensor_scalar(mean, mean, 1.0 / D, None, ALU.mult))
                    nc.vector.tensor_tensor(h1, x1_sup, over_d(mean), ALU.subtract).then_inc(centred, 1)
                    dve.wait_ge(centred, done(sup + 1))
                    link(nc.vector.tensor_tensor(square, h1, h1, ALU.mult))
                    link(nc.vector.tensor_reduce(out=var, in_=square, axis=AXX, op=ALU.add))
                    nc.vector.tensor_scalar(var, var, 1.0 / D, EPS, ALU.mult, ALU.add).then_inc(var_ready, 1)

                def scale(sup):
                    dve.wait_ge(v_chain, chain.n)
                    dve.wait_ge(dev_ready, done(sup + 1))
                    inverse_root(link, inv, var, t4)
                    nc.vector.scalar_tensor_tensor(out=h1, in0=h1, scalar=0.0, in1=over_d(inv),
                                                   op0=ALU.max, op1=ALU.mult).then_inc(h1_ready, 1)

                def take_wh(sup):
                    dve.wait_ge(projected, done(sup + 1))
                    dve.wait_ge(g_built, done(sup))
                    dve.wait_ge(wh_stored, sup * 16 + 16)
                    got = psum[:, 7, 0:SUP * (D + 2)].rearrange("p (k n) -> p k n", k=SUP)
                    nc.vector.tensor_copy(wh[:, :, 0:D], got[:, :, 0:D])
                    nc.vector.tensor_copy(s_col[:, bass.ds(sup * SUP, SUP)], got[:, :, D])
                    nc.vector.tensor_copy(d_col[:, bass.ds(sup * SUP, SUP)], got[:, :, D + 1])
                    nc.vector.tensor_scalar(d4, got[:, :, D + 1], SAFE, None, ALU.min).then_inc(wh_copied, 1)

                nc.vector.memset(wh[:, :, D:DE], 1.0)
                clamp(0, 0)
                norm_early(0)
                LINKS = 3 * 2 * NB + 4 + 5
                count = [0]

                def body(turn):
                    if not isinstance(turn, int):
                        chain.n = turn * LINKS + (count[0] - LINKS)
                    elif turn:
                        chain.n = count[0] + (TURNS - 2) * LINKS
                    for r in range(2 * NB):
                        if r < 2 * NB - 1:
                            clamp(turn, r + 1)
                        elif not last_turn(turn):
                            clamp(turn + 1, 0)
                        unpack(turn, r)
                        if first(turn):
                            if r == 0:
                                norm_early(1)
                            if r == 2:
                                prepare_weights()
                        elif r == 1:
                            centre(turn - 1)
                        elif r == 2:
                            scale(turn - 1)
                        elif r == 5:
                            take_wh(turn - 1)
                    if first(turn):
                        count[0] = chain.n

                def prepare_weights():
                    dve.wait_ge(wt_ready, 1)
                    nc.vector.tensor_copy(w_t, psum[0:D, 6, 0:D]).then_inc(wt_copied, 1)
                    dve.wait_ge(wa_ready, 1)
                    nc.vector.tensor_copy(w_cat[:, D:D + 2], psum[0:D, 7, 0:2]).then_inc(w_cat_ready, 1)

                turns(dve, body)
                last = NS - 1
                centre(last)
                scale(last)
                take_wh(last)
                dve.wait_ge(wh_copied, done(NS))
                link(nc.vector.tensor_reduce(out=d_abs[:, 0:1], in_=d_col[:, :], axis=AXX, op=ALU.max,
                                             apply_absolute_value=True))
                dve.sem_inc(d_abs_ready, 1)
                dve.wait_ge(g_built, done(NS))
                link(nc.vector.tensor_reduce(out=square[:, 0, :], in_=wh_sum.rearrange("p b d -> p d b"),
                                             axis=AXX, op=ALU.add))
                dve.sem_inc(mean_sum_ready, 1)
                dve.wait_ge(mean_ready, 1)
                nc.vector.tensor_scalar(wh_mean[:, :], psum[:, 6, 0:D], 1.0 / N, None, ALU.mult)
                dve.wait_ge(d_all_ready, 1)
                nc.vector.tensor_scalar(flag[:, :], d_abs[:, 1:2], SAFE, None, ALU.is_gt)

            @block.tensor
            def _(pe):
                pe.wait_ge(consts_ready, 1)
                for s in (packed, multiplied, turned, projected):
                    pe.sem_inc(s, HEAD)

                def pack(turn, r):
                    n = turn * (2 * NB) + r
                    pe.wait_ge(clamped, done(n * 2 + 2))
                    wait_apart(pe, evacuated, done(n + 1 - 4))
                    for t in range(HALF):
                        last = nc.tensor.matmul(psum[:, r % 4, t * W4:(t + 1) * W4],
                                                clamped_adj[:, r % 2, t, :], pack4[:, :], start=True, stop=True)
                    last.then_inc(packed, 1)

                def multiply(turn, r):
                    n = turn * (2 * NB) + r
                    bank = 4 + (r // 2) % 2
                    if r % 2 == 0:
                        pe.wait_ge(sum_copied, done(turn * NB + r // 2 + 1 - 2))
                    wait_apart(pe, unpacked, done(n + 1))
                    m8 = mask0[:, r % 2, :, :].bitcast(FP8)
                    for t in range(HALF):
                        tt = (r % 2) * HALF + t
                        last = nc.tensor.matmul(psum[:, bank, 0:3 * D], m8[:, t, :],
                                                h_parts[:, tt, :, :].rearrange("p c d -> p (c d)"),
                                                start=(tt == 0), stop=(tt == T - 1))
                    last.then_inc(multiplied, 1)

                def turn_h(sup):
                    pe.wait_ge(s_copied, done(sup))
                    wait_apart(pe, h1_ready, sup + 1)
                    for k in range(SUP):
                        last = nc.tensor.transpose(psum[0:D, 6, k * P:(k + 1) * P], h1[:, k, :], ident[:, :])
                    last.then_inc(turned, 1)

                def project(sup):
                    pe.wait_ge(wh_copied, done(sup))
                    pe.wait_ge(w_cat_ready, 1)
                    wait_apart(pe, h1_t_ready, done(sup + 1))
                    nc.tensor.matmul(psum[0:1, 6, :], w_cat[:, D:D + 1], h1_t, start=True, stop=True)
                    for k in range(SUP):
                        last = nc.tensor.matmul(psum[:, 7, k * (D + 2):(k + 1) * (D + 2)],
                                                h1_t[:, k * P:(k + 1) * P], w_cat[:, :], start=True, stop=True)
                    last.then_inc(projected, 1)

                def prepare_weights():
                    pe.wait_ge(w_in, 48)
                    pe.wait_ge(consts_ready, 2)
                    nc.tensor.transpose(psum[0:D, 6, 0:D], w_cat[:, 0:D], ident[0:D, 0:D]).then_inc(wt_ready, 1)
                    pe.wait_ge(wt_copied, 1)
                    nc.tensor.matmul(psum[0:D, 7, 0:2], w_t, a_two, start=True, stop=True).then_inc(wa_ready, 1)

                def body(turn):
                    for r in range(2 * NB):
                        if r < 2 * NB - 1:
                            pack(turn, r + 1)
                        elif not last_turn(turn):
                            pack(turn + 1, 0)
                        if first(turn) and r < 2:
                            pe.wait_ge(h_ready, r + 1)
                        multiply(turn, r)
                        if first(turn):
                            if r == 2:
                                prepare_weights()
                        elif r == 3:
                            turn_h(turn - 1)
                        elif r == 4:
                            project(turn - 1)

                pack(0, 0)
                turns(pe, body)
                pe.wait_ge(w_cat_ready, 1)
                turn_h(NS - 1)
                project(NS - 1)
                pe.wait_ge(s_copied, done(NS))
                pe.wait_ge(mean_sum_ready, 1)
                nc.tensor.matmul(psum[:, 6, 0:D], ones[:, :], square[:, 0, :], start=True, stop=True).then_inc(mean_ready, 1)

            @block.scalar
            def _(act):
                for s in (evacuated, sum_copied, dev_ready, h1_t_ready, s_copied, exp_ready):
                    act.sem_inc(s, HEAD)
                act.sem_inc(s_stored, 16)
                act.sem_inc(wh_stored, 16)
                act.dma_start(w_cat[:, 0:D], weight_w).then_inc(w_in, 16)
                with nc.allow_non_contiguous_dma(reason="128 numbers"):
                    act.dma_start(a_two, weight_a.rearrange("(k o) c -> o (k c)", k=2)).then_inc(w_in, 16)
                act.dma_start(bias_b[:, :], bias.rearrange("(a d) -> a d", a=1).broadcast_to([P, D])).then_inc(w_in, 16)
                act.dma_start(x_sup, x_sups[0]).then_inc(x_landed, 16)

                def norm_early(k):
                    dst = h_all[:, k]
                    parts = h_parts[:, k * HALF:(k + 1) * HALF]
                    act.wait_ge(ln_v, 4 * k + 1)
                    nc.scalar.activation(sq_all, dst, ACT.Square).then_inc(ln_a, 1)
                    act.wait_ge(ln_v, 4 * k + 2)
                    nc.scalar.activation(st_all[:, 1, :], st_all[:, 2, :], ACT.Sqrt).then_inc(ln_a, 1)
                    act.wait_ge(ln_v, 4 * k + 3)
                    nc.scalar.activation(parts[:, :, 0, :], dst, ACT.Copy).then_inc(ln_a, 1)
                    act.wait_ge(ln_v, 4 * k + 4)
                    nc.scalar.activation(parts[:, :, 1, :], sq_all, ACT.Copy).then_inc(ln_a, 1)

                def evacuate(turn, r):
                    n = turn * (2 * NB) + r
                    act.wait_ge(packed, done(n + 1))
                    act.wait_ge(unpacked, done(n + 1 - 4))
                    nc.scalar.activation(words4[:, r % 4, :, :].rearrange("p t w -> p (t w)"),
                                         psum[:, r % 4, :], ACT.Copy).then_inc(evacuated, 1)

                def copy_sum(turn, r):
                    b = turn * NB + r // 2
                    act.wait_ge(multiplied, done(turn * (2 * NB) + r + 1))
                    act.wait_ge(sum_added, done(b + 1 - 2))
                    nc.scalar.activation(l0_sum[:, (r // 2) % 2, :, :].rearrange("p c d -> p (c d)"),
                                         psum[:, 4 + (r // 2) % 2, 0:3 * D], ACT.Copy, scale=0.5
                                         ).then_inc(sum_copied, 1)

                def store_x1(sup):
                    act.wait_ge(sum_added, done(sup * SUP + SUP))
                    act.dma_start(x1_sups[sup], x1_sup).then_inc(x1_stored, 16)

                def root(sup):
                    act.wait_ge(var_ready, sup + 1)
                    nc.scalar.activation(small[:, 1, :], small[:, 2, :], ACT.Sqrt).then_inc(dev_ready, 1)

                def copy_turned(sup):
                    act.wait_ge(turned, done(sup + 1))
                    act.wait_ge(projected, done(sup))
                    nc.scalar.activation(h1_t, psum[0:D, 6, :], ACT.Copy).then_inc(h1_t_ready, 1)

                def copy_s(sup):
                    act.wait_ge(projected, done(sup + 1))
                    act.wait_ge(s_stored, sup * 16 + 16)
                    nc.scalar.activation(s_row[:, :], psum[0:1, 6, :], ACT.Copy).then_inc(s_copied, 1)
                    act.wait_ge(s_copied, done(sup + 1))
                    act.dma_start(s_sups[sup], s_row[:, :]).then_inc(s_stored, 16)

                def take_exps(sup):
                    act.wait_ge(wh_copied, done(sup + 1))
                    act.wait_ge(g_built, done(sup))
                    nc.scalar.activation(exps[:, 0, :], small[:, 4, :], ACT.Exp)
                    nc.scalar.activation(exps[:, 1, :], small[:, 4, :], ACT.Exp, scale=SLOPE).then_inc(exp_ready, 1)
                    act.dma_start(wh_sups[sup], wh[:, :, 0:D]).then_inc(wh_stored, 16)

                def body(turn):
                    sup = turn - 1
                    for r in range(2 * NB):
                        if r < 2 * NB - 1:
                            evacuate(turn, r + 1)
                        elif not last_turn(turn):
                            evacuate(turn + 1, 0)
                        if first(turn) and r == 0:
                            norm_early(1)
                        if r % 2 == 1:
                            copy_sum(turn, r)
                        if r == 6 and not last_turn(turn):
                            act.wait_ge(base_built, turn + 1)
                            act.dma_start(x_sup, x_sups[turn + 1]).then_inc(x_landed, 16)
                        if first(turn):
                            continue
                        if r == 0:
                            store_x1(sup)
                        elif r == 1:
                            root(sup)
                        elif r == 3:
                            copy_turned(sup)
                        elif r == 4:
                            copy_s(sup)
                        elif r == 5:
                            take_exps(sup)

                evacuate(0, 0)
                norm_early(0)
                turns(act, body)
                last = NS - 1
                store_x1(last)
                root(last)
                copy_turned(last)
                copy_s(last)
                take_exps(last)

            @block.gpsimd
            def _(pool):
                chain = Chain(pool, p_chain, wait_apart)
                link = chain.link
                pool.sem_inc(sum_added, HEAD)
                pool.sem_inc(g_built, HEAD)
                link(nc.gpsimd.memset(pack4[:, :], 0.0))
                for k in range(4):
                    for e in range(2):
                        link(nc.gpsimd.affine_select(
                            out=pack4[:, :], in_=pack4[:, :], compare_op=ALU.not_equal,
                            fill=float(4 ** (k + 4 * e)), base=-(32 * k + e), pattern=[[-2, W4]],
                            channel_multiplier=1))
                pool.sem_inc(consts_ready, 1)
                nc.gpsimd.memset(wh_sum, 0.0)
                nc.gpsimd.memset(ones[:, :], 1.0)
                link(nc.gpsimd.memset(ident[:, :], 0.0))
                link(nc.gpsimd.affine_select(out=ident[:, :], in_=ident[:, :], compare_op=ALU.not_equal,
                                             fill=1.0, base=0, pattern=[[-1, P]], channel_multiplier=1))
                pool.sem_inc(consts_ready, 1)
                pool.wait_ge(h_ready, 2)

                def base(turn):
                    wait_apart(pool, x_landed, turn * 16 + 16)
                    if not first(turn):
                        pool.wait_ge(centred, done(turn))
                        wait_apart(pool, x1_stored, turn * 16)
                    hp = h_parts[:, bass.ds(turn * SUP, SUP), :, :]
                    for c in range(3):
                        ins = nc.gpsimd.tensor_tensor(x1_sup, x_sup if c == 0 else x1_sup, hp[:, :, c, :], ALU.add)
                        link(ins)
                    pool.sem_inc(base_built, 1)

                def add_sum(turn, r):
                    pool.wait_ge(sum_copied, done(turn * NB + r + 1))
                    a = l0_sum[:, r % 2, :, :]
                    link(nc.gpsimd.tensor_tensor(a[:, 1, :], a[:, 1, :], a[:, 2, :], ALU.add))
                    link(nc.gpsimd.tensor_tensor(a[:, 0, :], a[:, 0, :], a[:, 1, :], ALU.add))
                    xb = x1_sup[:, r, :]
                    nc.gpsimd.tensor_tensor(xb, xb, a[:, 0, :], ALU.add).then_inc(sum_added, 1)

                def build(sup):
                    pool.wait_ge(exp_ready, done(sup + 1))
                    for g in range(2):
                        last = nc.gpsimd.tensor_tensor(g_full[:, g], wh, exps[:, g, :].unsqueeze(2).broadcast_to([P, SUP, DE]), ALU.mult)
                    link(last)
                    gp = gparts[:, bass.ds(sup * SUP, SUP), :, :, :].rearrange("p t g c d -> p g t c d")
                    for c in range(2):
                        for g in range(2):
                            last = nc.gpsimd.tensor_copy(gp[:, g, :, c, :], g_full[:, g])
                        link(last)
                        for g in range(2):
                            to = g_full[:, g] if c == 0 else gp[:, g, :, 2, :]
                            last = nc.gpsimd.tensor_tensor(to, g_full[:, g], gp[:, g, :, c, :], ALU.subtract)
                        link(last)
                    nc.gpsimd.tensor_tensor(wh_sum, wh_sum, wh[:, :, 0:D], ALU.add).then_inc(g_built, 1)

                LINKS = 3 + 2 * NB + 5
                count = [0]

                def body(turn):
                    if not isinstance(turn, int):
                        chain.n = turn * LINKS + (count[0] - LINKS)
                    elif turn:
                        chain.n = count[0] + (TURNS - 2) * LINKS
                    base(turn)
                    for r in range(NB):
                        add_sum(turn, r)
                        if r == 2 and not first(turn):
                            build(turn - 1)
                    if first(turn):
                        count[0] = chain.n

                turns(pool, body)
                build(NS - 1)
                pool.wait_ge(d_abs_ready, 1)
                nc.gpsimd.partition_all_reduce(d_abs[:, 1:2], d_abs[:, 0:1], P, RMAX).then_inc(d_all_ready, 1)

        signs_ready, low_ready, masks_ready = sem("signs_ready"), sem("low_ready"), sem("masks_ready")
        chunk_done, first_copied, sums_ready = sem("chunk_done"), sem("first_copied"), sem("sums_ready")
        rows_out, out_done, l1_v, l1_p = sem("rows_out"), sem("out_done"), sem("l1_v"), sem("l1_p")
        den_ready, rec_ready = sem("den_ready"), sem("rec_ready")
        gen_v, gen_turned, gen_mdiag, gen_m = sem("gen_v"), sem("gen_turned"), sem("gen_mdiag"), sem("gen_m")
        gen_max, gen_z, gen_exp, gen_e, gen_sum = (
            sem("gen_max"), sem("gen_z"), sem("gen_exp"), sem("gen_e"), sem("gen_sum"))
        gen_rows = sem("gen_rows")
        HC = CT // 2
        s_in, x1_in = [sem("s_in0"), sem("s_in1")], [sem("x1_in0"), sem("x1_in1")]
        gen_in, factors_in, factors_ready = sem("gen_in"), sem("factors_in"), sem("factors_ready")
        fin = sb("fin", [P, SUP, 3], F32)

        with nc.Block() as block:
            @block.sync
            def _(sp):
                general = sp.value_load(flag[0:1, 0:1], min_val=0, max_val=1)
                with sp.If(general == 0):
                    def load_s(s, par):
                        sp.dma_start(s_rows[:, par, :], s_sups[s].broadcast_to([P, SUPW])).then_inc(s_in[par], 16)

                    def load_x1(s, par):
                        sp.dma_start(x1_back[:, par], x1_sups[s]).then_inc(x1_in[par], 16)

                    def rows(s, par, more):
                        if more:
                            sp.wait_ge(signs_ready, done(s * (2 * NCH) + 2 * NCH))
                            load_s(s + 2, par)
                        sp.wait_ge(rows_out, done(s + 1))
                        sp.dma_start(out_rows[s], x1_back[:, par]).then_inc(out_done, 16)
                        if more:
                            sp.wait_ge(out_done, s * 16 + 16)
                            load_x1(s + 2, par)

                    for par in range(2):
                        load_s(par, par)
                        load_x1(par, par)
                    with sp.Fori(0, NS // 2 - 1) as pair:
                        for par in range(2):
                            rows(pair * 2 + par, par, True)
                    for par in range(2):
                        rows(NS - 2 + par, par, False)
                with sp.Else():
                    sp.dma_start(s_rows_all, s_dram.broadcast_to([P, N])).then_inc(gen_in, 16)
                    sp.dma_start(wh_all[:, :, 0:D], wh_dram.rearrange("t q d -> q t d")).then_inc(gen_in, 16)
                    sp.dma_start(x1_all, x1_dram.rearrange("t q d -> q t d")).then_inc(gen_in, 16)
                    with sp.Fori(0, NS) as s:
                        sp.wait_ge(gen_rows, done(s * SUP + SUP))
                        sp.dma_start(out_rows[s], x1_all[:, bass.ds(s * SUP, SUP), :]).then_inc(out_done, 16)
                sp.wait_ge(out_done, 16 * NS)

            @block.scalar
            def _(act):
                general = act.value_load(flag[0:1, 0:1], min_val=0, max_val=1)
                with act.If(general == 0):
                    act.sem_inc(signs_ready, HEAD)
                    act.sem_inc(first_copied, HEAD)

                    def signs(s, h, par):
                        u = s * (2 * NCH) + h
                        if h == 0:
                            wait_apart(act, s_in[par], (s - par) * 8 + 16)
                        wait_apart(act, low_ready, done(u + 1 - 2))
                        for k in range(HC):
                            t = h * HC + k
                            last = nc.scalar.activation(sign[:, h % 2, k, :], s_rows[:, par, :],
                                                        ACT.Sign, bias=d_col[:, t:t + 1])
                        last.then_inc(signs_ready, 1)

                    def copy_first(s, par):
                        act.wait_ge(chunk_done, done(s * NCH + NCH))
                        act.wait_ge(rows_out, done(s))
                        src = psum[:, 4 * par:4 * par + SUP, 0:6 * DE].rearrange("p b (g c d) -> p b g c d", g=2, c=3)
                        for g in range(2):
                            last = nc.scalar.activation(sums[:, :, g, :], src[:, :, g, 0, :], ACT.Copy)
                        last.then_inc(first_copied, 1)

                    for h in range(4):
                        signs(0, h, 0)
                    act.wait_ge(factors_in, 1)
                    nc.scalar.activation(alpha, alpha, ACT.Exp, scale=1.0 - SLOPE)
                    nc.scalar.activation(beta, beta, ACT.Exp, scale=SLOPE - 1.0).then_inc(factors_ready, 1)
                    with act.Fori(0, NS // 2 - 1) as pair:
                        for par in range(2):
                            s = pair * 2 + par
                            for h in range(4, 2 * NCH):
                                signs(s, h, par)
                            for h in range(4):
                                signs(s + 1, h, 1 - par)
                            copy_first(s, par)
                    for par in range(2):
                        s = NS - 2 + par
                        for h in range(4, 2 * NCH):
                            signs(s, h, par)
                        if par == 0:
                            for h in range(4):
                                signs(s + 1, h, 1 - par)
                        copy_first(s, par)
                with act.Else():
                    with act.Fori(0, T) as b:
                        act.wait_ge(gen_z, b + 1)
                        nc.scalar.activation(z_all, z_all, ACT.Exp).then_inc(gen_exp, 1)

            @block.vector
            def _(dve):
                general = dve.value_load(flag[0:1, 0:1], min_val=0, max_val=1)
                with dve.If(general == 0):
                    dve.sem_inc(low_ready, HEAD)
                    dve.sem_inc(masks_ready, HEAD)

                    def chunk(s, c):
                        v = s * NCH + c
                        slot = c % 2
                        dve.wait_ge(chunk_done, done(v + 1 - 2))
                        w16 = words[:, s, c * CT:(c + 1) * CT, :, :].rearrange("p t b w -> p (t b w)").bitcast(
                            U16).rearrange("p (n w) -> p n w", w=W1)
                        e16 = edges[:, slot, :, :].rearrange("p t i -> p (t i)").bitcast(U16)
                        l16 = low[:, slot, :, :].rearrange("p t i -> p (t i)").bitcast(U16)
                        e_view = e16.rearrange("p (n m w) -> p n m w", m=8, w=W1)
                        for m in range(8):
                            op, by = (ALU.logical_shift_left, 6 - m) if m <= 6 else (ALU.logical_shift_right, 1)
                            last = nc.vector.tensor_scalar(e_view[:, :, m, :], w16, by, 0x4040, op, ALU.bitwise_and)
                        last.then_inc(l1_v, 1)
                        dve.wait_ge(l1_v, v + 1)
                        n2 = HC * SUPW // 2
                        for k in range(2):
                            h = 2 * c + k
                            u = s * (2 * NCH) + h
                            dve.wait_ge(signs_ready, done(u + 1))
                            part = slice(k * n2, (k + 1) * n2)
                            g16 = sign[:, h % 2, :, :].rearrange("p t i -> p (t i)").bitcast(U16)
                            nc.vector.tensor_tensor(l16[:, part], e16[:, part], g16, ALU.bitwise_and
                                                    ).then_inc(low_ready, 1)
                        for k in range(2):
                            u = s * (2 * NCH) + 2 * c + k
                            part = slice(k * n2, (k + 1) * n2)
                            dve.wait_ge(low_ready, done(u + 1))
                            nc.vector.tensor_tensor(e16[:, part], e16[:, part], l16[:, part], ALU.bitwise_xor
                                                    ).then_inc(masks_ready, 1)

                    def add_parts(s, par):
                        src = psum[:, 4 * par:4 * par + SUP, 0:6 * DE].rearrange("p b (g c d) -> p b g c d", g=2, c=3)
                        dve.wait_ge(first_copied, done(s + 1))
                        for g in range(2):
                            last = nc.vector.tensor_tensor(sums[:, :, g, :], sums[:, :, g, :], src[:, :, g, 1, :], ALU.add)
                        last.then_inc(sums_ready, 1)
                        dve.wait_ge(sums_ready, s * 2 + 1)
                        for g in range(2):
                            last = nc.vector.tensor_tensor(sums[:, :, g, :], sums[:, :, g, :], src[:, :, g, 2, :], ALU.add)
                        last.then_inc(sums_ready, 1)

                    def invert(s):
                        dve.wait_ge(den_ready, s + 1)
                        nc.vector.reciprocal(fin[:, :, 2], fin[:, :, 1]).then_inc(rec_ready, 1)

                    nc.vector.tensor_scalar(alpha, s_col[:, :], 0.0, None, ALU.min)
                    nc.vector.tensor_scalar(beta, s_col[:, :], 0.0, None, ALU.max).then_inc(factors_in, 1)
                    chunk(0, 0)
                    chunk(0, 1)
                    with dve.Fori(0, NS // 2 - 1) as pair:
                        for par in range(2):
                            s = pair * 2 + par
                            for c in range(2, NCH):
                                chunk(s, c)
                            chunk(s + 1, 0)
                            chunk(s + 1, 1)
                            add_parts(s, par)
                            invert(s)
                    for par in range(2):
                        s = NS - 2 + par
                        for c in range(2, NCH):
                            chunk(s, c)
                        if par == 0:
                            chunk(s + 1, 0)
                            chunk(s + 1, 1)
                        add_parts(s, par)
                        invert(s)
                with dve.Else():
                    dve.sem_inc(gen_rows, HEAD)
                    STEPS = 19
                    w_view = words[:, :, :, :, :]
                    dve.wait_ge(gen_in, 48)
                    nc.vector.memset(wh_all[:, :, D:DE], 1.0)
                    nc.vector.tensor_tensor(x1_all, x1_all, bias_b[:, :].unsqueeze(1).broadcast_to([P, T, D]),
                                            ALU.add).then_inc(gen_v, 1)
                    dve.wait_ge(gen_v, 1)
                    with dve.Fori(0, NS) as s:
                        for k in range(SUP):
                            b = s * SUP + k
                            count = [0]

                            def link(ins):
                                count[0] += 1
                                ins.then_inc(gen_v, 1)
                                wait_apart(dve, gen_v, b * STEPS + count[0] + 1)

                            e16 = edges1.rearrange("p t i -> p (t i)").bitcast(U16).rearrange(
                                "p (n m w) -> p n m w", m=8, w=W1)
                            w16 = w_view[:, s, :, k, :].bitcast(U16)
                            dve.wait_ge(gen_rows, done(b))
                            for m in range(8):
                                op, by = (ALU.logical_shift_left, 6 - m) if m <= 6 else (ALU.logical_shift_right, 1)
                                last = nc.vector.tensor_scalar(e16[:, :, m, :], w16, by, 0x4040, op, ALU.bitwise_and)
                            link(last)
                            e8 = edges1.bitcast(FP8)
                            link(nc.vector.tensor_scalar(tmp, d_col[:, :], d_abs[:, 1:2], None, ALU.add))
                            link(nc.vector.tensor_tensor(z_all, e8, tmp.unsqueeze(2).broadcast_to([P, T, P]), ALU.mult))
                            link(nc.vector.tensor_reduce(out=row_max, in_=z_all.rearrange("p t i -> p i t"),
                                                         axis=AXX, op=ALU.max))
                            dve.sem_inc(gen_max, 1)
                            dve.wait_ge(gen_turned, b + 1)
                            link(nc.vector.tensor_reduce(out=m_cols[:, 0:1], in_=psum[:, 0, 0:P], axis=AXX, op=ALU.max))
                            link(nc.vector.tensor_scalar(m_cols[:, 0:1], m_cols[:, 0:1], 0.5, d_abs[:, 1:2],
                                                         ALU.mult, ALU.subtract))
                            link(nc.vector.tensor_tensor(m_cols[:, 0:1], m_cols[:, 0:1], s_col[:, bass.ds(b, 1)], ALU.add))
                            link(nc.vector.scalar_tensor_tensor(out=m_cols[:, 1:2], in0=m_cols[:, 0:1], scalar=SLOPE,
                                                                in1=m_cols[:, 0:1], op0=ALU.mult, op1=ALU.max))
                            link(nc.vector.tensor_scalar(m_diag, ident[:, :], m_cols[:, 1:2], None, ALU.mult))
                            dve.sem_inc(gen_mdiag, 1)
                            link(nc.vector.tensor_tensor(
                                z_all, s_rows_all[:, bass.ds(b * P, P)].unsqueeze(1).broadcast_to([P, T, P]),
                                d_col[:, :].unsqueeze(2).broadcast_to([P, T, P]), ALU.add))
                            link(nc.vector.scalar_tensor_tensor(out=z_all, in0=z_all, scalar=SLOPE, in1=z_all,
                                                                op0=ALU.mult, op1=ALU.max))
                            dve.wait_ge(gen_m, b + 1)
                            link(nc.vector.tensor_tensor(
                                z_all, z_all, psum[:, 1, 0:P].unsqueeze(1).broadcast_to([P, T, P]), ALU.subtract))
                            link(nc.vector.tensor_scalar(z_all, z_all, 0.0, None, ALU.min))
                            dve.sem_inc(gen_z, 1)
                            wait_apart(dve, gen_exp, b + 1)
                            link(nc.vector.tensor_tensor(z_all, z_all, e8, ALU.mult))
                            dve.sem_inc(gen_e, 1)
                            dve.wait_ge(gen_sum, b + 1)
                            link(nc.vector.tensor_copy(out1, psum[:, 2, 0:DE]))
                            link(nc.vector.tensor_scalar(m_cols[:, 2:3], out1[:, D:DE], 0.0, None, ALU.is_equal))
                            link(nc.vector.scalar_tensor_tensor(out=out1[:, 0:D], in0=wh_mean[:, :], scalar=m_cols[:, 2:3],
                                                                in1=out1[:, 0:D], op0=ALU.mult, op1=ALU.add))
                            link(nc.vector.tensor_tensor(out1[:, D:DE], out1[:, D:DE], m_cols[:, 2:3], ALU.add))
                            link(nc.vector.reciprocal(m_cols[:, 3:4], out1[:, D:DE]))
                            xb = x1_all[:, b, :]
                            nc.vector.scalar_tensor_tensor(out=xb, in0=out1[:, 0:D], scalar=m_cols[:, 3:4], in1=xb,
                                                           op0=ALU.mult, op1=ALU.add).then_inc(gen_rows, 1)
                            assert count[0] == STEPS

            @block.tensor
            def _(pe):
                general = pe.value_load(flag[0:1, 0:1], min_val=0, max_val=1)
                with pe.If(general == 0):
                    pe.sem_inc(chunk_done, HEAD)
                    with pe.Fori(0, NS // 2) as pair:
                        for par in range(2):
                            s = pair * 2 + par
                            pe.wait_ge(first_copied, done(s + 1 - 2))
                            for c in range(NCH):
                                v = s * NCH + c
                                for t in range(CT):
                                    if t % HC == 0:
                                        wait_apart(pe, masks_ready, done(v * 2 + t // HC + 1))
                                    tt = c * CT + t
                                    for b in range(SUP):
                                        for g, m in ((0, edges), (1, low)):
                                            last = nc.tensor.matmul(
                                                psum[:, 4 * par + b, g * 3 * DE:(g + 1) * 3 * DE],
                                                m[:, c % 2, t, b * P:(b + 1) * P].bitcast(FP8),
                                                gparts[:, tt, g, :, :].rearrange("p c d -> p (c d)"),
                                                start=(tt == 0 and g == 0), stop=(tt == T - 1),
                                                skip_group_check=True)
                                last.then_inc(chunk_done, 1)
                with pe.Else():
                    with pe.Fori(0, T) as b:
                        pe.wait_ge(gen_max, b + 1)
                        nc.tensor.transpose(psum[:, 0, 0:P], row_max, ident[:, :]).then_inc(gen_turned, 1)
                        pe.wait_ge(gen_mdiag, b + 1)
                        nc.tensor.matmul(psum[:, 1, 0:P], ones[:, :], m_diag, start=True, stop=True).then_inc(gen_m, 1)
                        pe.wait_ge(gen_e, b + 1)
                        for t in range(T):
                            last = nc.tensor.matmul(psum[:, 2, 0:DE], z_all[:, t, :], wh_all[:, t, :],
                                                    start=(t == 0), stop=(t == T - 1))
                        last.then_inc(gen_sum, 1)

            @block.gpsimd
            def _(pool):
                general = pool.value_load(flag[0:1, 0:1], min_val=0, max_val=1)
                with pool.If(general == 0):
                    STEPS = 8
                    pool.sem_inc(rows_out, HEAD)
                    pool.wait_ge(factors_ready, 1)
                    def finish(s, par):
                        count = [0]

                        def link(ins):
                            count[0] += 1
                            ins.then_inc(l1_p, 1)
                            wait_apart(pool, l1_p, s * STEPS + count[0])

                        wait_apart(pool, sums_ready, s * 2 + 2)
                        for g, f in ((0, alpha), (1, beta)):
                            last = nc.gpsimd.tensor_tensor(
                                sums[:, :, g, :], sums[:, :, g, :],
                                f[:, bass.ds(s * SUP, SUP)].unsqueeze(2).broadcast_to([P, SUP, DE]), ALU.mult)
                        link(last)
                        num = sums[:, :, 0, :]
                        link(nc.gpsimd.tensor_tensor(num, num, sums[:, :, 1, :], ALU.add))
                        link(nc.gpsimd.tensor_scalar(fin[:, :, 0], num[:, :, D], 0.0, None, ALU.is_equal))
                        link(nc.gpsimd.tensor_tensor(fin[:, :, 1], num[:, :, D], fin[:, :, 0], ALU.add))
                        pool.sem_inc(den_ready, 1)
                        link(nc.gpsimd.tensor_tensor(
                            sums[:, :, 1, 0:D], wh_mean[:, :].unsqueeze(1).broadcast_to([P, SUP, D]),
                            fin[:, :, 0].unsqueeze(2).broadcast_to([P, SUP, D]), ALU.mult))
                        link(nc.gpsimd.tensor_tensor(num[:, :, 0:D], num[:, :, 0:D], sums[:, :, 1, 0:D], ALU.add))
                        pool.wait_ge(rec_ready, s + 1)
                        link(nc.gpsimd.tensor_tensor(num[:, :, 0:D], num[:, :, 0:D],
                                                     fin[:, :, 2].unsqueeze(2).broadcast_to([P, SUP, D]), ALU.mult))
                        xb = x1_back[:, par]
                        pool.wait_ge(x1_in[par], (s - par) * 8 + 16)
                        link(nc.gpsimd.tensor_tensor(xb, xb, bias_b[:, :].unsqueeze(1).broadcast_to([P, SUP, D]),
                                                     ALU.add))
                        nc.gpsimd.tensor_tensor(xb, xb, num[:, :, 0:D], ALU.add).then_inc(rows_out, 1)
                        assert count[0] == STEPS

                    with pool.Fori(0, NS // 2) as pair:
                        for par in range(2):
                            finish(pair * 2 + par, par)


def kernel(x, adj, L1_gnn_weight_w, L1_gnn_weight_a, L1_gnn_bias):
    import numpy as np
    import concourse.bacc as bacc
    from concourse.bass_utils import run_bass_kernel_spmd

    nc = bacc.Bacc("TRN2", target_bir_lowering=False, num_devices=1)
    arrays, args = {}, []
    for name, a in (("x", x), ("adj", adj), ("weight_w", L1_gnn_weight_w),
                    ("weight_a", L1_gnn_weight_a), ("bias", L1_gnn_bias)):
        a = np.ascontiguousarray(a)
        arrays[name] = a
        args.append(nc.dram_tensor(name, a.shape, mybir.dt.from_np(a.dtype), kind="ExternalInput").ap())
    args.append(nc.dram_tensor("out", x.shape, mybir.dt.float32, kind="ExternalOutput").ap())
    gnn_two_layers(nc, *args)
    r = run_bass_kernel_spmd(nc, [arrays], core_ids=[0])
    return r.results[0]["out"]
```

```python
import concourse.bass as bass
import concourse.mybir as mybir
from contextlib import ExitStack

F32 = mybir.dt.float32
BF16 = mybir.dt.bfloat16
FP8 = mybir.dt.float8e4
I32 = mybir.dt.int32
I8 = mybir.dt.int8
U8 = mybir.dt.uint8
U16 = mybir.dt.uint16
U32 = mybir.dt.uint32
ALU = mybir.AluOpType
ACT = mybir.ActivationFunctionType
AXX = mybir.AxisListType.X
RMAX = bass.bass_isa.ReduceOp.max


def gnn_two_layers(
    nc: bass.Bass,
    x: bass.AP,
    adj: bass.AP,
    weight_w: bass.AP,
    weight_a: bass.AP,
    bias: bass.AP,
    out: bass.AP,
):
    N, D = x.shape
    P = 128
    T = N // P
    HALF = T // 2
    SUP = 4
    NS = T // SUP
    W4 = P // 8
    W1 = P // 16
    DE = D + 1
    SUPW = SUP * P
    CT = 16
    NCH = T // CT
    NE = 8
    T0 = CT // SUP + 1
    SAFE = 50.0
    SLOPE = 0.01
    EPS = 1e-5
    KB = 1024
    HEAD = 4

    def done(k):
        return k + HEAD

    ctx = ExitStack()
    with ctx:
        def sb(name, shape, dt):
            return ctx.enter_context(nc.sbuf_tensor(name, shape, dt))

        def sem(name):
            return ctx.enter_context(nc.semaphore(name))

        words = sb("words", [P, NS, T, SUP, W1 // 2], U32)
        g_flat = sb("gparts", [P, T * 2 * 3 * DE], BF16)
        gparts = g_flat[:, :].rearrange("p (t g c d) -> p t g c d", t=T, g=2, c=3)
        arena = sb("arena", [P, 88 * KB], U8)
        ident = sb("ident", [P, P], F32)
        ones = sb("ones", [P, P], F32)
        pack4 = sb("pack4", [P, W4], BF16)
        s_col = sb("s_col", [P, T], F32)
        d_col = sb("d_col", [P, T], F32)
        w_cat = sb("w_cat", [D, D + 2], F32)
        wh_mean = sb("wh_mean", [P, D], F32)
        bias_b = sb("bias_b", [P, D], F32)
        flag = sb("flag", [P, 1], I32)
        d_abs = sb("d_abs", [P, 2], F32)
        psum = ctx.enter_context(nc.psum_tensor("psum", [P, 8, 512], F32))
        x1_dram = nc.dram_tensor("x1_rows", [NS, P, SUP * D], F32, kind="Internal").ap()
        wh_dram = nc.dram_tensor("wh_rows", [NS, P, SUP * D], F32, kind="Internal").ap()
        partial_dram = nc.dram_tensor("partial_sums", [NE, P, SUP * 2 * DE], F32, kind="Internal").ap()
        s_dram = nc.dram_tensor("s_row", [1, N], F32, kind="Internal").ap()
        waited = {e.engine: sem(f"waited_{n}") for n, e in
                  (("act", nc.scalar), ("dve", nc.vector), ("pe", nc.tensor), ("pool", nc.gpsimd))}

        def region(lo, size, dt):
            return arena[:, lo:lo + size].bitcast(dt)

        QUART = N // 4
        adj_in = region(0, 32 * KB, I32).rearrange("p (s n) -> p s n", s=4)
        clamped_adj = region(32 * KB, 8 * KB, FP8).rearrange("p (s t i) -> p s t i", s=2, t=HALF)
        words4 = region(40 * KB, 4 * KB, U16).rearrange("p (s t w) -> p s t w", s=4, t=HALF)
        mask0 = region(44 * KB, 8 * KB, U8).rearrange("p (s t i) -> p s t i", s=2, t=HALF)
        h_parts = region(52 * KB, 24 * KB, BF16).rearrange("p (t c d) -> p t c d", t=T, c=3)
        any4 = region(76 * KB, HALF * W4 * 2, U32).rearrange("p (t w) -> p t w", t=HALF)
        l0_sum = region(77 * KB, 6 * D * 4, F32).rearrange("p (s c d) -> p s c d", s=2, c=3)
        SD = SUP * D * 4

        def super_rows(lo):
            return region(lo, SD, F32).rearrange("p (b d) -> p b d", b=SUP)

        x_sup, x1_sup = super_rows(79 * KB), super_rows(80 * KB)
        h1, square = super_rows(81 * KB), super_rows(82 * KB)
        h1_t = region(83 * KB, 2 * KB, F32)[0:D]
        wh = region(85 * KB, SUP * DE * 4, F32).rearrange("p (b d) -> p b d", b=SUP)
        wh_sum = super_rows(86 * KB + 64)
        small = region(87 * KB + 64, 8 * SUP * 4, F32).rearrange("p (k b) -> p k b", k=8)
        s_row = sb("s_row_sb", [1, SUPW], F32)
        g_full = sb("g_full", [P, 2, SUP, DE], F32)
        w_t = region(87 * KB + 256, D * 4, F32)[0:D]
        a_two = region(87 * KB + 512, 8, F32)[0:D]
        exps = region(87 * KB + 576, 2 * SUP * 4, F32).rearrange("p (g b) -> p g b", g=2)
        early = g_flat[:, :].bitcast(F32)
        HD = HALF * D
        x_all = early[:, 0:2 * HD].rearrange("p (k t d) -> p k t d", k=2, t=HALF)
        h_all = early[:, 2 * HD:4 * HD].rearrange("p (k t d) -> p k t d", k=2, t=HALF)
        sq_all = [early[:, 4 * HD:5 * HD].rearrange("p (t d) -> p t d", t=HALF), x_all[:, 0]]
        st_all = early[:, 5 * HD:5 * HD + 8 * HALF].rearrange("p (h k t) -> p h k t", h=2, k=4)
        edges = region(0, 16 * KB, U8).rearrange("p (s t i) -> p s t i", s=2, t=CT)
        low = region(16 * KB, 16 * KB, U8).rearrange("p (s t i) -> p s t i", s=2, t=CT)
        sign = region(32 * KB, 8 * KB, I8).rearrange("p (s t i) -> p s t i", s=2, t=CT // 2)
        sums = region(52 * KB, SUP * 2 * DE * 4, F32).rearrange("p (b g d) -> p b g d", b=SUP, g=2)
        s_rows = region(40 * KB, 4 * KB, F32).rearrange("p (s i) -> p s i", s=2)
        x1_back = region(59 * KB, 2 * KB, F32).rearrange("p (s b d) -> p s b d", s=2, b=SUP)
        factors = region(61 * KB, 2 * T * 4, F32).rearrange("p (t g) -> p t g", g=2)
        partial_back = region(54 * KB + 256, SUP * 2 * DE * 4 * 2, F32).rearrange("p (s n) -> p s n", s=2)
        assert T0 + NE <= NS - 3 and NE % 2 == 0

        def unfilled(sup):
            return words[:, sup, :, :, :].rearrange("p t b w -> p (t b w)").bitcast(U8).rearrange(
                "p (t i) -> p t i", t=CT)

        pair_edges, pair_low = unfilled(NS - 3), unfilled(NS - 2)
        tail = early[:, (NS - 4) * SUP * 3 * DE:]
        pair_s = tail[:, 0:2 * 2 * P].rearrange("p (n i) -> p n i", n=2)
        tail = tail[:, 2 * 2 * P:]
        pair_acc = tail[:, 0:12 * DE].rearrange("p (n c d) -> p n c d", n=4, c=3)
        pair_sums = tail[:, 12 * DE:16 * DE].rearrange("p (n d) -> p n d", n=4)
        pair_sign = [unfilled(NS - 1).bitcast(I8), tail[:, 16 * DE:16 * DE + CT * 2 * P // 4].bitcast(I8).rearrange(
            "p (t i) -> p t i", t=CT)]
        z_all = early[:, 0:T * P].rearrange("p (t i) -> p t i", t=T)
        edges1 = region(0, 8 * KB, U8).rearrange("p (t i) -> p t i", t=T)
        wh_all = region(8 * KB, T * DE * 4, F32).rearrange("p (t d) -> p t d", t=T)
        s_rows_all = region(50 * KB, 32 * KB, F32)
        row_max = region(26 * KB, P * 4, F32)
        m_diag = region(27 * KB, P * 4, F32)
        m_cols = region(28 * KB, 4 * 4, F32)
        out1 = region(29 * KB, DE * 4, F32)
        tmp = region(30 * KB, T * 4, F32)
        x1_all = region(32 * KB, 16 * KB, F32).rearrange("p (t d) -> p t d", t=T)

        x_rows = x.rearrange("(t q) d -> q t d", q=P)
        out_rows = out.rearrange("(s b q) d -> s q b d", q=P, b=SUP)
        adj_rows = adj.rearrange("(b q) j -> b q j", q=P)
        x_sups = x.rearrange("(s b q) d -> s q b d", q=P, b=SUP)
        x1_sups = x1_dram.rearrange("s q (b d) -> s q b d", b=SUP)
        wh_sups = wh_dram.rearrange("s q (b d) -> s q b d", b=SUP)
        s_pairs = s_dram.rearrange("a (s j i) -> s j a i", j=2, i=2 * P)
        s_sups = s_dram.rearrange("a (s i) -> s a i", i=SUPW)

        def wait_apart(eng, s, value):
            eng.wait_ge(s, value)
            eng.sem_inc(waited[eng.engine], 1)

        class Chain:

            def __init__(self, eng, s, wait=None):
                self.eng, self.sem, self.n = eng, s, 0
                self.wait = wait or (lambda e, s, value: e.wait_ge(s, value))

            def link(self, ins):
                ins.then_inc(self.sem, 1)
                self.n = self.n + 1
                self.wait(self.eng, self.sem, self.n)

        def inverse_root(link, inv, var, t):
            link(nc.vector.reciprocal(inv, inv))
            link(nc.vector.tensor_tensor(t, inv, inv, ALU.mult))
            link(nc.vector.tensor_tensor(t, t, var, ALU.mult))
            link(nc.vector.tensor_scalar(t, t, -0.5, 1.5, ALU.mult, ALU.add))
            link(nc.vector.tensor_tensor(inv, inv, t, ALU.mult))

        x_in = [sem("x_in0"), sem("x_in1")]
        adj_landed = [sem(f"adj_landed{k}") for k in range(4)]
        clamped, packed, evacuated = sem("clamped"), sem("packed"), sem("evacuated")
        unpacked, multiplied = sem("unpacked"), sem("multiplied")
        sum_copied, sum_added = sem("sum_copied"), sem("sum_added")
        consts_ready, v_chain, p_chain = sem("consts_ready"), sem("v_chain"), sem("p_chain")
        ln_v, ln_a = [sem("ln_v0"), sem("ln_v1")], [sem("ln_a0"), sem("ln_a1")]
        ln_mean, rest_ready = sem("ln_mean"), sem("rest_ready")
        h_ready = [sem("h_ready0"), sem("h_ready1")]
        w_in, wt_ready, wt_copied = sem("w_in"), sem("wt_ready"), sem("wt_copied")
        wa_ready, w_cat_ready = sem("wa_ready"), sem("w_cat_ready")
        centred, var_ready, dev_ready, h1_ready = sem("centred"), sem("var_ready"), sem("dev_ready"), sem("h1_ready")
        turned, h1_t_ready, projected = sem("turned"), sem("h1_t_ready"), sem("projected")
        s_copied, wh_copied, exp_ready, g_built = sem("s_copied"), sem("wh_copied"), sem("exp_ready"), sem("g_built")
        x_landed, base_built = sem("x_landed"), sem("base_built")
        x1_stored, wh_stored, s_stored = sem("x1_stored"), sem("wh_stored"), sem("s_stored")
        d_abs_ready, d_all_ready, mean_sum_ready, mean_ready = (
            sem("d_abs_ready"), sem("d_all_ready"), sem("mean_sum_ready"), sem("mean_ready"))
        NB = SUP
        TURNS = T // NB

        def turns(eng, body, between=None):
            body(0)
            with eng.Fori(1, T0) as turn:
                body(turn)
            with eng.Fori(T0, T0 + NE) as turn:
                body(turn, [(turn - T0, j) for j in range(2)])
            if between:
                between()
            with eng.Fori(T0 + NE, TURNS - 1) as turn:
                body(turn)
            body(TURNS - 1)

        SIGN_AT, SPREAD_AT, SPLIT_AT = ((0, 1), (2, 3)), (0, 4), (2, 5)
        MULTIPLY_AT, COPY_AT, STORE_AT, ADD_AT = ((3, 4), (6, 7)), (4, 7), (6, 8), (2, 3)

        def first(turn):
            return isinstance(turn, int) and turn == 0

        def last_turn(turn):
            return isinstance(turn, int) and turn == TURNS - 1

        signs_ready, low_ready, masks_ready = sem("signs_ready"), sem("low_ready"), sem("masks_ready")
        chunk_done, first_copied, sums_ready = sem("chunk_done"), sem("first_copied"), sem("sums_ready")
        rows_out, out_done, l1_v = sem("rows_out"), sem("out_done"), sem("l1_v")
        edges_ready, biased = sem("edges_ready"), sem("biased")
        gen_v, gen_turned, gen_mdiag, gen_m = sem("gen_v"), sem("gen_turned"), sem("gen_mdiag"), sem("gen_m")
        gen_max, gen_z, gen_exp, gen_e, gen_sum = (
            sem("gen_max"), sem("gen_z"), sem("gen_exp"), sem("gen_e"), sem("gen_sum"))
        gen_rows = sem("gen_rows")
        s_in, x1_in = [sem("s_in0"), sem("s_in1")], [sem("x1_in0"), sem("x1_in1")]
        gen_in, factors_in, factors_ready = sem("gen_in"), sem("factors_in"), sem("factors_ready")
        pair_s_in, pair_signs, pair_edges_ready, pair_low_ready, pair_masks = (
            sem("pair_s_in"), sem("pair_signs"), sem("pair_edges"), sem("pair_low"), sem("pair_masks"))
        pair_done, pair_copied, pair_chain, pair_added, pair_stored = (
            sem("pair_done"), sem("pair_copied"), sem("pair_chain"), sem("pair_added"), sem("pair_stored"))
        partial_in, mean_taken = [sem("partial_in0"), sem("partial_in1")], sem("mean_taken")
        HC = CT // 2
        NH = 2 * NCH

        def order(s, par, c, lo):
            if lo:
                return s * (NCH - 1) + c - 1, (par * (NCH - 1) + c - 1) % 2
            return s * NCH + c - NE, (c + NE) % 2

        def load_s(sp, s, par):
            sp.dma_start(s_rows[:, par, :], s_sups[s].broadcast_to([P, SUPW])).then_inc(s_in[par], 16)

        def signs(act, s, par, h, lo):
            v, _ = order(s, par, h // 2, lo)
            if h == 2 * lo:
                wait_apart(act, s_in[par], (s - par) * 8 + 16)
            wait_apart(act, low_ready, done(v * 2 + h % 2 + 1 - 2))
            for k in range(HC):
                t = h * HC + k
                last = nc.scalar.activation(sign[:, h % 2, k, :], s_rows[:, par, :],
                                            ACT.Sign, bias=d_col[:, t:t + 1])
            last.then_inc(signs_ready, 1)

        def spread(dve, e16, w16):
            for m in range(8):
                op, by = (ALU.logical_shift_left, 6 - m) if m <= 6 else (ALU.logical_shift_right, 1)
                last = nc.vector.tensor_scalar(e16[m], w16, by, 0x4040, op, ALU.bitwise_and)
            return last

        def edges_of(dve, s, par, c, lo):
            v, slot = order(s, par, c, lo)
            dve.wait_ge(chunk_done, done(v + 1 - 2))
            w16 = words[:, s, c * CT:(c + 1) * CT, :, :].rearrange("p t b w -> p (t b w)").bitcast(
                U16).rearrange("p (n w) -> p n w", w=W1)
            e_view = edges[:, slot, :, :].rearrange("p t i -> p (t i)").bitcast(U16).rearrange(
                "p (n m w) -> p n m w", m=8, w=W1)
            spread(dve, [e_view[:, :, m, :] for m in range(8)], w16).then_inc(edges_ready, 1)

        def split(dve, s, par, h, lo):
            v, slot = order(s, par, h // 2, lo)
            u, n2 = v * 2 + h % 2, HC * SUPW // 2
            part = slice((h % 2) * n2, (h % 2 + 1) * n2)
            e16 = edges[:, slot, :, :].rearrange("p t i -> p (t i)").bitcast(U16)[:, part]
            l16 = low[:, slot, :, :].rearrange("p t i -> p (t i)").bitcast(U16)[:, part]
            g16 = sign[:, h % 2, :, :].rearrange("p t i -> p (t i)").bitcast(U16)
            dve.wait_ge(edges_ready, v + 1)
            dve.wait_ge(signs_ready, done(u + 1))
            nc.vector.tensor_tensor(l16, e16, g16, ALU.bitwise_and).then_inc(low_ready, 1)
            dve.wait_ge(low_ready, done(u + 1))
            nc.vector.tensor_tensor(e16, e16, l16, ALU.bitwise_xor).then_inc(masks_ready, 1)

        def chunk(dve, s, par, c, lo):
            edges_of(dve, s, par, c, lo)
            split(dve, s, par, 2 * c, lo)
            split(dve, s, par, 2 * c + 1, lo)

        def multiply1(pe, s, par, h, lo):
            v, slot = order(s, par, h // 2, lo)
            wait_apart(pe, masks_ready, done(v * 2 + h % 2 + 1))
            for k in range(HC):
                tt = h * HC + k
                for b in range(SUP):
                    for g, m in ((0, edges), (1, low)):
                        last = nc.tensor.matmul(
                            psum[:, 4 * par + b, g * 3 * DE:(g + 1) * 3 * DE],
                            m[:, slot, (h % 2) * HC + k, b * P:(b + 1) * P].bitcast(FP8),
                            gparts[:, tt, g, :, :].rearrange("p c d -> p (c d)"),
                            start=(tt == lo * CT and g == 0), stop=(tt == T - 1), skip_group_check=True)
            if h % 2 == 1:
                last.then_inc(chunk_done, 1)

        with nc.Block() as block:
            @block.sync
            def _(sp):
                for k in range(2):
                    sp.dma_start(x_all[:, k], x_rows[:, k * HALF:(k + 1) * HALF, :]).then_inc(x_in[k], 16)

                def body(turn, pairs=()):
                    if pairs:
                        sup, j = pairs[0]
                        sp.wait_ge(s_stored, pairs[-1][0] * 16 + 32)
                        sp.wait_ge(pair_signs, done(sup * 2 + j))
                    for n, (sup, j) in enumerate(pairs):
                        sp.dma_start(pair_s[:, n, :], s_pairs[sup, j].broadcast_to([P, 2 * P])
                                     ).then_inc(pair_s_in, 16)
                    for m in range(4 * NB):
                        sp.wait_ge(clamped, done(turn * (4 * NB) + m + 1 - 4))
                        sp.dma_start(adj_in[:, m % 4, :],
                                     adj_rows[turn * NB + m // 4, :, (m % 4) * QUART:(m % 4 + 1) * QUART]
                                     ).then_inc(adj_landed[m % 4], 16)
                turns(sp, body)
                for s in range(2):
                    sp.wait_ge(unpacked, done(2 * T - 2 + 2 * s))
                    load_s(sp, s, s)
                sp.wait_ge(x1_stored, 16 * NS)
                sp.wait_ge(wh_stored, 16 * NS + 16)
                sp.wait_ge(s_stored, 16 * NS + 16)

            @block.vector
            def _(dve):
                for s in (clamped, unpacked, centred, wh_copied, low_ready, masks_ready, pair_low_ready):
                    dve.sem_inc(s, HEAD)
                chain = Chain(dve, v_chain)
                link = chain.link

                def norm_early(stage, k):
                    dst, square_k = h_all[:, k], sq_all[k]
                    mean, inv, var, t = (st_all[:, k, n, :] for n in range(4))
                    parts = h_parts[:, k * HALF:(k + 1) * HALF]

                    def over_d(v):
                        return v.unsqueeze(2).broadcast_to([P, HALF, D])
                    if stage == 0:
                        dve.wait_ge(x_in[k], 16)
                        link(nc.vector.tensor_reduce(out=mean, in_=x_all[:, k], axis=AXX, op=ALU.add))
                        if k == 0:
                            link(nc.vector.tensor_scalar(mean, mean, 1.0 / D, None, ALU.mult))
                            nc.vector.tensor_tensor(dst, x_all[:, k], over_d(mean), ALU.subtract).then_inc(ln_v[k], 1)
                        else:
                            nc.vector.tensor_scalar(mean, mean, 1.0 / D, None, ALU.mult).then_inc(ln_mean, 1)
                    elif stage == 1:
                        dve.wait_ge(ln_a[k], 1)
                        link(nc.vector.tensor_reduce(out=var, in_=square_k, axis=AXX, op=ALU.add))
                        nc.vector.tensor_scalar(var, var, 1.0 / D, EPS, ALU.mult, ALU.add).then_inc(ln_v[k], 1)
                    elif stage == 2:
                        dve.wait_ge(ln_a[k], 2)
                        inverse_root(link, inv, var, t)
                        nc.vector.scalar_tensor_tensor(out=dst, in0=dst, scalar=0.0, in1=over_d(inv),
                                                       op0=ALU.max, op1=ALU.mult).then_inc(ln_v[k], 1)
                    elif stage == 3:
                        dve.wait_ge(ln_a[k], 3)
                        nc.vector.tensor_tensor(square_k, dst, parts[:, :, 0, :], ALU.subtract).then_inc(ln_v[k], 1)
                    else:
                        dve.wait_ge(ln_a[k], 4)
                        nc.vector.tensor_tensor(parts[:, :, 2, :], square_k, parts[:, :, 1, :], ALU.subtract
                                                ).then_inc(h_ready[k], 1)

                def clamp(turn, r):
                    n = turn * (2 * NB) + r
                    wait_apart(dve, packed, done(n + 1 - 2))
                    for q in range(2):
                        wait_apart(dve, adj_landed[2 * (r % 2) + q], (turn * NB + (r // 2 + 1)) * 16)
                        nc.vector.tensor_scalar(
                            clamped_adj[:, r % 2, q * HALF // 2:(q + 1) * HALF // 2, :].rearrange("p t i -> p (t i)"),
                            adj_in[:, 2 * (r % 2) + q, :],
                            0.0, 2.0, ALU.max, ALU.min, saturate=False).then_inc(clamped, 1)

                def unpack(turn, r):
                    n = turn * (2 * NB) + r
                    dve.wait_ge(evacuated, done(n + 1))
                    dve.wait_ge(multiplied, done(n + 1 - 2))
                    dve.wait_ge(v_chain, chain.n)
                    w32 = words4[:, r % 4, :, :].rearrange("p t w -> p (t w)").bitcast(U32)
                    m16 = mask0[:, r % 2, :, :].rearrange("p t i -> p (t i)").bitcast(U16).rearrange(
                        "p (t k w) -> p t k w", t=HALF, k=4)
                    nc.vector.scalar_tensor_tensor(
                        out=any4.rearrange("p t w -> p (t w)"), in0=w32, scalar=1, in1=w32,
                        op0=ALU.logical_shift_right, op1=ALU.bitwise_or).then_inc(v_chain, 1)
                    for k in range(4):
                        last = nc.vector.tensor_scalar(
                            m16[:, :, k, :], words4[:, r % 4, :, :], 6 - 2 * k, 0x4040,
                            ALU.logical_shift_left, ALU.bitwise_and)
                    last.then_inc(unpacked, 1)
                    chain.n = chain.n + 1
                    dve.wait_ge(v_chain, chain.n)
                    link(nc.vector.tensor_scalar(any4, any4, 0x55555555, None, ALU.bitwise_and))
                    hs = slice((r % 2) * HALF, (r % 2 + 1) * HALF)
                    nc.vector.scalar_tensor_tensor(
                        out=words[:, turn, hs, r // 2, :],
                        in0=any4[:, :, W1 // 2:W1], scalar=1, in1=any4[:, :, 0:W1 // 2],
                        op0=ALU.logical_shift_left, op1=ALU.bitwise_or).then_inc(v_chain, 1)
                    chain.n = chain.n + 1

                mean, inv, var, t4, d4 = (small[:, n, :] for n in range(5))

                def over_d(v):
                    return v.unsqueeze(2).broadcast_to([P, SUP, D])

                def centre(sup):
                    dve.wait_ge(sum_added, done(sup * SUP + SUP))
                    dve.wait_ge(turned, done(sup))
                    dve.wait_ge(v_chain, chain.n)
                    link(nc.vector.tensor_reduce(out=mean, in_=x1_sup, axis=AXX, op=ALU.add))
                    link(nc.vector.tensor_scalar(mean, mean, 1.0 / D, None, ALU.mult))
                    nc.vector.tensor_tensor(h1, x1_sup, over_d(mean), ALU.subtract).then_inc(centred, 1)
                    dve.wait_ge(centred, done(sup + 1))
                    link(nc.vector.tensor_tensor(square, h1, h1, ALU.mult))
                    link(nc.vector.tensor_reduce(out=var, in_=square, axis=AXX, op=ALU.add))
                    nc.vector.tensor_scalar(var, var, 1.0 / D, EPS, ALU.mult, ALU.add).then_inc(var_ready, 1)

                def scale(sup):
                    dve.wait_ge(v_chain, chain.n)
                    dve.wait_ge(dev_ready, done(sup + 1))
                    inverse_root(link, inv, var, t4)
                    nc.vector.scalar_tensor_tensor(out=h1, in0=h1, scalar=0.0, in1=over_d(inv),
                                                   op0=ALU.max, op1=ALU.mult).then_inc(h1_ready, 1)

                def take_wh(sup):
                    dve.wait_ge(projected, done(sup + 1))
                    dve.wait_ge(g_built, done(sup))
                    dve.wait_ge(wh_stored, sup * 16 + 16)
                    got = psum[:, 7, 0:SUP * (D + 2)].rearrange("p (k n) -> p k n", k=SUP)
                    nc.vector.tensor_copy(wh[:, :, 0:D], got[:, :, 0:D])
                    nc.vector.tensor_copy(s_col[:, bass.ds(sup * SUP, SUP)], got[:, :, D])
                    nc.vector.tensor_copy(d_col[:, bass.ds(sup * SUP, SUP)], got[:, :, D + 1])
                    nc.vector.tensor_scalar(d4, got[:, :, D + 1], SAFE, None, ALU.min).then_inc(wh_copied, 1)

                nc.vector.memset(wh[:, :, D:DE], 1.0)
                for stage, k in ((0, 0), (0, 1), (1, 0)):
                    norm_early(stage, k)
                clamp(0, 0)
                for stage, k in ((2, 0), (1, 1)):
                    norm_early(stage, k)
                clamp(0, 1)
                norm_early(2, 1)
                LINKS = 3 * 2 * NB + 4 + 5
                count = [0]

                def body(turn, pairs=()):
                    if not isinstance(turn, int):
                        chain.n = turn * LINKS + (count[0] - LINKS)
                    elif turn:
                        chain.n = count[0] + (TURNS - 2) * LINKS
                    for r in range(2 * NB):
                        if r < 2 * NB - 1:
                            if not (first(turn) and r == 0):
                                clamp(turn, r + 1)
                        elif not last_turn(turn):
                            clamp(turn + 1, 0)
                        unpack(turn, r)
                        if first(turn):
                            if r < 2:
                                norm_early((3, 4)[r], 1)
                            if r == 3:
                                take_turned_weights()
                            if r == 6:
                                take_w_a()
                        elif r == 1:
                            centre(turn - 1)
                        elif r == 2:
                            scale(turn - 1)
                        elif r == 5:
                            take_wh(turn - 1)
                        for n, (sup, j) in enumerate(pairs):
                            if r == SPREAD_AT[n]:
                                spread_pair(sup, j)
                            if r == SPLIT_AT[n]:
                                split_pair(sup, j)
                    if first(turn):
                        count[0] = chain.n

                e16 = pair_edges.rearrange("p t i -> p (t i)").bitcast(U16)
                l16 = pair_low.rearrange("p t i -> p (t i)").bitcast(U16)

                def spread_pair(sup, j):
                    dve.wait_ge(pair_done, done(sup * 2 + j))
                    e_view = e16.rearrange("p (t b m w) -> p t b m w", b=2, m=8, w=W1)
                    w_pair = words[:, sup, 0:CT, 2 * j:2 * j + 2, :].bitcast(U16)
                    spread(dve, [e_view[:, :, :, m, :] for m in range(8)], w_pair).then_inc(pair_edges_ready, 1)

                def split_pair(sup, j):
                    u = sup * 2 + j
                    dve.wait_ge(pair_edges_ready, u + 1)
                    dve.wait_ge(pair_signs, done(u + 1))
                    g16 = pair_sign[j].rearrange("p t i -> p (t i)").bitcast(U16)
                    nc.vector.tensor_tensor(l16, e16, g16, ALU.bitwise_and).then_inc(pair_low_ready, 1)
                    dve.wait_ge(pair_low_ready, done(u + 1))
                    nc.vector.tensor_tensor(e16, e16, l16, ALU.bitwise_xor).then_inc(pair_masks, 1)

                def between():
                    dve.wait_ge(pair_done, done(2 * NE))

                def take_turned_weights():
                    dve.wait_ge(wt_ready, 1)
                    nc.vector.tensor_copy(w_t, psum[0:D, 6, 0:D]).then_inc(wt_copied, 1)

                def take_w_a():
                    dve.wait_ge(wa_ready, 1)
                    nc.vector.tensor_copy(w_cat[:, D:D + 2], psum[0:D, 7, 0:2]).then_inc(w_cat_ready, 1)

                turns(dve, body, between)
                edges_of(dve, 0, 0, 1, 1)
                split(dve, 0, 0, 2, 1)
                centre(NS - 1)
                split(dve, 0, 0, 3, 1)
                scale(NS - 1)
                edges_of(dve, 0, 0, 2, 1)
                split(dve, 0, 0, 4, 1)
                take_wh(NS - 1)
                dve.wait_ge(wh_copied, done(NS))
                link(nc.vector.tensor_reduce(out=d_abs[:, 0:1], in_=d_col[:, :], axis=AXX, op=ALU.max,
                                             apply_absolute_value=True))
                dve.sem_inc(d_abs_ready, 1)
                split(dve, 0, 0, 5, 1)
                edges_of(dve, 0, 0, 3, 1)
                split(dve, 0, 0, 6, 1)
                dve.wait_ge(g_built, done(NS))
                link(nc.vector.tensor_reduce(out=square[:, 0, :], in_=wh_sum.rearrange("p b d -> p d b"),
                                             axis=AXX, op=ALU.add))
                dve.sem_inc(mean_sum_ready, 1)
                split(dve, 0, 0, 7, 1)
                edges_of(dve, 1, 1, 1, 1)
                split(dve, 1, 1, 2, 1)
                dve.wait_ge(mean_ready, 1)
                nc.vector.tensor_scalar(wh_mean[:, :], psum[:, 6, 0:D], 1.0 / N, None, ALU.mult).then_inc(mean_taken, 1)
                dve.wait_ge(d_all_ready, 1)
                nc.vector.tensor_scalar(flag[:, :], d_abs[:, 1:2], SAFE, None, ALU.is_gt)
                split(dve, 1, 1, 3, 1)
                chunk(dve, 1, 1, 2, 1)

            @block.tensor
            def _(pe):
                pe.wait_ge(consts_ready, 1)
                for s in (packed, multiplied, turned, projected, chunk_done, pair_done):
                    pe.sem_inc(s, HEAD)

                def pack(turn, r):
                    n = turn * (2 * NB) + r
                    pe.wait_ge(clamped, done(n * 2 + 2))
                    wait_apart(pe, evacuated, done(n + 1 - 2))
                    for t in range(HALF):
                        last = nc.tensor.matmul(psum[:, r % 2, t * W4:(t + 1) * W4],
                                                clamped_adj[:, r % 2, t, :], pack4[:, :], start=True, stop=True)
                    last.then_inc(packed, 1)

                def multiply(turn, r):
                    n = turn * (2 * NB) + r
                    bank = 4 + (r // 2) % 2
                    if r % 2 == 0:
                        pe.wait_ge(sum_copied, done(turn * NB + r // 2 + 1 - 2))
                    wait_apart(pe, unpacked, done(n + 1))
                    m8 = mask0[:, r % 2, :, :].bitcast(FP8)
                    for t in range(HALF):
                        tt = (r % 2) * HALF + t
                        last = nc.tensor.matmul(psum[:, bank, 0:3 * D], m8[:, t, :],
                                                h_parts[:, tt, :, :].rearrange("p c d -> p (c d)"),
                                                start=(tt == 0), stop=(tt == T - 1))
                    last.then_inc(multiplied, 1)

                def turn_h(sup):
                    pe.wait_ge(s_copied, done(sup))
                    wait_apart(pe, h1_ready, sup + 1)
                    for k in range(SUP):
                        last = nc.tensor.transpose(psum[0:D, 6, k * P:(k + 1) * P], h1[:, k, :], ident[:, :])
                    last.then_inc(turned, 1)

                def project(sup):
                    pe.wait_ge(wh_copied, done(sup))
                    pe.wait_ge(w_cat_ready, 1)
                    wait_apart(pe, h1_t_ready, done(sup + 1))
                    nc.tensor.matmul(psum[0:1, 6, :], w_cat[:, D:D + 1], h1_t, start=True, stop=True)
                    for k in range(SUP):
                        last = nc.tensor.matmul(psum[:, 7, k * (D + 2):(k + 1) * (D + 2)],
                                                h1_t[:, k * P:(k + 1) * P], w_cat[:, :], start=True, stop=True)
                    last.then_inc(projected, 1)

                def turn_weights():
                    pe.wait_ge(w_in, 48)
                    pe.wait_ge(consts_ready, 2)
                    nc.tensor.transpose(psum[0:D, 6, 0:D], w_cat[:, 0:D], ident[0:D, 0:D]).then_inc(wt_ready, 1)

                def project_a():
                    pe.wait_ge(wt_copied, 1)
                    nc.tensor.matmul(psum[0:D, 7, 0:2], w_t, a_two, start=True, stop=True).then_inc(wa_ready, 1)

                def multiply_pair(sup, j, half):
                    u = sup * 2 + j
                    if half == 0:
                        pe.wait_ge(pair_copied, done(u))
                        wait_apart(pe, pair_masks, u + 1)
                    for t in range(half * HC, (half + 1) * HC):
                        for b in range(2):
                            for g, m in ((0, pair_edges), (1, pair_low)):
                                last = nc.tensor.matmul(
                                    psum[:, 2 + b, g * 3 * DE:(g + 1) * 3 * DE],
                                    m[:, t, b * P:(b + 1) * P].bitcast(FP8),
                                    gparts[:, t, g, :, :].rearrange("p c d -> p (c d)"),
                                    start=(t == 0 and g == 0), stop=(t == CT - 1), skip_group_check=True)
                    if half == 1:
                        last.then_inc(pair_done, 1)

                def body(turn, pairs=()):
                    for r in range(2 * NB):
                        pair_products(pairs, r)
                        if r < 2 * NB - 1:
                            pack(turn, r + 1)
                        elif not last_turn(turn):
                            pack(turn + 1, 0)
                        if first(turn) and r < 2:
                            pe.wait_ge(h_ready[r], 1)
                        multiply(turn, r)
                        if first(turn):
                            if r == 2:
                                turn_weights()
                            if r == 4:
                                project_a()
                        elif r == 3:
                            turn_h(turn - 1)
                        elif r == 4:
                            project(turn - 1)

                def pair_products(pairs, r):
                    for n, (sup, j) in enumerate(pairs):
                        for half in range(2):
                            if r == MULTIPLY_AT[n][half]:
                                multiply_pair(sup, j, half)

                pack(0, 0)
                turns(pe, body)
                pe.wait_ge(w_cat_ready, 1)
                multiply1(pe, 0, 0, 2, 1)
                turn_h(NS - 1)
                multiply1(pe, 0, 0, 3, 1)
                project(NS - 1)
                for h in range(4, 7):
                    multiply1(pe, 0, 0, h, 1)
                pe.wait_ge(s_copied, done(NS))
                pe.wait_ge(mean_sum_ready, 1)
                nc.tensor.matmul(psum[:, 6, 0:D], ones[:, :], square[:, 0, :], start=True, stop=True
                                 ).then_inc(mean_ready, 1)
                multiply1(pe, 0, 0, 7, 1)
                pe.wait_ge(mean_taken, 1)
                for h in range(2, 4):
                    multiply1(pe, 1, 1, h, 1)

            @block.scalar
            def _(act):
                for s in (evacuated, sum_copied, dev_ready, h1_t_ready, s_copied, exp_ready, signs_ready, first_copied,
                          pair_signs, pair_copied):
                    act.sem_inc(s, HEAD)
                act.sem_inc(s_stored, 16)
                act.sem_inc(wh_stored, 16)
                act.sem_inc(pair_stored, 16)
                act.dma_start(w_cat[:, 0:D], weight_w).then_inc(w_in, 16)
                with nc.allow_non_contiguous_dma(reason="128 numbers"):
                    act.dma_start(a_two, weight_a.rearrange("(k o) c -> o (k c)", k=2)).then_inc(w_in, 16)
                act.dma_start(bias_b[:, :], bias.rearrange("(a d) -> a d", a=1).broadcast_to([P, D])).then_inc(w_in, 16)
                act.dma_start(x_sup, x_sups[0]).then_inc(x_landed, 16)

                def norm_early(stage, k):
                    parts = h_parts[:, k * HALF:(k + 1) * HALF]
                    if stage == 3 and k == 0:
                        act.wait_ge(rest_ready, 1)
                    else:
                        act.wait_ge(ln_v[k], stage + 1)
                    if stage == 0:
                        nc.scalar.activation(sq_all[k], h_all[:, k], ACT.Square).then_inc(ln_a[k], 1)
                    elif stage == 1:
                        nc.scalar.activation(st_all[:, k, 1, :], st_all[:, k, 2, :], ACT.Sqrt).then_inc(ln_a[k], 1)
                    elif stage == 2:
                        nc.scalar.activation(parts[:, :, 0, :], h_all[:, k], ACT.Copy).then_inc(ln_a[k], 1)
                    else:
                        nc.scalar.activation(parts[:, :, 1, :], sq_all[k], ACT.Copy).then_inc(ln_a[k], 1)

                def evacuate(turn, r):
                    n = turn * (2 * NB) + r
                    act.wait_ge(packed, done(n + 1))
                    act.wait_ge(unpacked, done(n + 1 - 4))
                    nc.scalar.activation(words4[:, r % 4, :, :].rearrange("p t w -> p (t w)"),
                                         psum[:, r % 2, :], ACT.Copy).then_inc(evacuated, 1)

                def copy_sum(turn, r):
                    b = turn * NB + r // 2
                    act.wait_ge(multiplied, done(turn * (2 * NB) + r + 1))
                    act.wait_ge(sum_added, done(b + 1 - 2))
                    nc.scalar.activation(l0_sum[:, (r // 2) % 2, :, :].rearrange("p c d -> p (c d)"),
                                         psum[:, 4 + (r // 2) % 2, 0:3 * D], ACT.Copy, scale=0.5
                                         ).then_inc(sum_copied, 1)

                def store_x1(sup):
                    act.wait_ge(sum_added, done(sup * SUP + SUP))
                    act.dma_start(x1_sups[sup], x1_sup).then_inc(x1_stored, 16)

                def root(sup):
                    act.wait_ge(var_ready, sup + 1)
                    nc.scalar.activation(small[:, 1, :], small[:, 2, :], ACT.Sqrt).then_inc(dev_ready, 1)

                def copy_turned(sup):
                    act.wait_ge(turned, done(sup + 1))
                    act.wait_ge(projected, done(sup))
                    nc.scalar.activation(h1_t, psum[0:D, 6, :], ACT.Copy).then_inc(h1_t_ready, 1)

                def copy_s(sup):
                    act.wait_ge(projected, done(sup + 1))
                    act.wait_ge(s_stored, sup * 16 + 16)
                    nc.scalar.activation(s_row[:, :], psum[0:1, 6, :], ACT.Copy).then_inc(s_copied, 1)
                    act.wait_ge(s_copied, done(sup + 1))
                    act.dma_start(s_sups[sup], s_row[:, :]).then_inc(s_stored, 16)

                def take_exps(sup):
                    act.wait_ge(wh_copied, done(sup + 1))
                    act.wait_ge(g_built, done(sup))
                    nc.scalar.activation(exps[:, 0, :], small[:, 4, :], ACT.Exp)
                    nc.scalar.activation(exps[:, 1, :], small[:, 4, :], ACT.Exp, scale=SLOPE).then_inc(exp_ready, 1)
                    act.dma_start(wh_sups[sup], wh[:, :, 0:D]).then_inc(wh_stored, 16)

                def sign_pair(pairs, n, half):
                    sup, j = pairs[n]
                    if half == 0 and n == 0:
                        wait_apart(act, pair_s_in, (sup * 2 + j + len(pairs)) * 16)
                    if half == 0:
                        wait_apart(act, pair_low_ready, done(sup * 2 + j + 1 - 2))
                    for t in range(half * HC, (half + 1) * HC):
                        last = nc.scalar.activation(pair_sign[j][:, t, :], pair_s[:, n, :],
                                                    ACT.Sign, bias=d_col[:, t:t + 1])
                    if half == 1:
                        last.then_inc(pair_signs, 1)

                def copy_pair(sup, j):
                    u = sup * 2 + j
                    wait_apart(act, pair_done, done(u + 1))
                    wait_apart(act, pair_added, done(u))
                    nc.scalar.activation(pair_acc.rearrange("p (b g) c d -> p b (g c d)", b=2),
                                         psum[:, 2:4, 0:6 * DE], ACT.Copy).then_inc(pair_copied, 1)

                def store_pair(sup, j):
                    act.wait_ge(pair_added, done(sup * 2 + j + 1))
                    act.dma_start(partial_dram[sup][:, j * 4 * DE:(j + 1) * 4 * DE],
                                  pair_sums.rearrange("p n d -> p (n d)")).then_inc(pair_stored, 16)

                def body(turn, pairs=()):
                    sup = turn - 1
                    for r in range(2 * NB):
                        if r < 2 * NB - 1:
                            evacuate(turn, r + 1)
                        elif not last_turn(turn):
                            evacuate(turn + 1, 0)
                        pair_copies(pairs, r)
                        if first(turn) and r == 0:
                            for stage, k in ((2, 1), (3, 1)):
                                norm_early(stage, k)
                        if last_turn(turn) and r == 6:
                            signs(act, 0, 0, 2, 1)
                        if r % 2 == 1:
                            copy_sum(turn, r)
                        if r == 6 and not last_turn(turn):
                            act.wait_ge(base_built, turn + 1)
                            act.dma_start(x_sup, x_sups[turn + 1]).then_inc(x_landed, 16)
                        if first(turn):
                            continue
                        if r == 0:
                            store_x1(sup)
                        elif r == 1:
                            root(sup)
                        elif r == 3:
                            copy_turned(sup)
                        elif r == 4:
                            copy_s(sup)
                        elif r == 5:
                            take_exps(sup)
                        pair_steps(pairs, r)
                    pair_steps(pairs, 2 * NB)

                def pair_copies(pairs, r):
                    for n, (sup, j) in enumerate(pairs):
                        if r == COPY_AT[n]:
                            copy_pair(sup, j)

                def pair_steps(pairs, r):
                    for n, (sup, j) in enumerate(pairs):
                        for half in range(2):
                            if r == SIGN_AT[n][half]:
                                sign_pair(pairs, n, half)
                        if r == STORE_AT[n]:
                            store_pair(sup, j)

                for stage, k in ((0, 0), (1, 0), (0, 1)):
                    norm_early(stage, k)
                evacuate(0, 0)
                for stage, k in ((2, 0), (1, 1), (3, 0)):
                    norm_early(stage, k)
                turns(act, body)
                store_x1(NS - 1)
                signs(act, 0, 0, 3, 1)
                root(NS - 1)
                signs(act, 0, 0, 4, 1)
                copy_turned(NS - 1)
                signs(act, 0, 0, 5, 1)
                copy_s(NS - 1)
                take_exps(NS - 1)
                for h in range(6, NH):
                    signs(act, 0, 0, h, 1)
                for h in range(2, 6):
                    signs(act, 1, 1, h, 1)

            @block.gpsimd
            def _(pool):
                chain = Chain(pool, p_chain, wait_apart)
                link = chain.link
                pool.sem_inc(sum_added, HEAD)
                pool.sem_inc(g_built, HEAD)
                pool.sem_inc(pair_added, HEAD)
                link(nc.gpsimd.memset(pack4[:, :], 0.0))
                for k in range(4):
                    for e in range(2):
                        link(nc.gpsimd.affine_select(
                            out=pack4[:, :], in_=pack4[:, :], compare_op=ALU.not_equal,
                            fill=float(4 ** (k + 4 * e)), base=-(32 * k + e), pattern=[[-2, W4]],
                            channel_multiplier=1))
                pool.sem_inc(consts_ready, 1)
                nc.gpsimd.memset(wh_sum, 0.0)
                nc.gpsimd.memset(ones[:, :], 1.0)
                link(nc.gpsimd.memset(ident[:, :], 0.0))
                link(nc.gpsimd.affine_select(out=ident[:, :], in_=ident[:, :], compare_op=ALU.not_equal,
                                             fill=1.0, base=0, pattern=[[-1, P]], channel_multiplier=1))
                pool.sem_inc(consts_ready, 1)
                pool.wait_ge(x_in[1], 16)
                pool.wait_ge(ln_mean, 1)
                nc.gpsimd.tensor_tensor(h_all[:, 1], x_all[:, 1], st_all[:, 1, 0, :].unsqueeze(2).broadcast_to(
                    [P, HALF, D]), ALU.subtract).then_inc(ln_v[1], 1)
                early_parts = h_parts[:, 0:HALF]
                pool.wait_ge(ln_a[0], 3)
                nc.gpsimd.tensor_tensor(sq_all[0], h_all[:, 0], early_parts[:, :, 0, :], ALU.subtract
                                        ).then_inc(rest_ready, 1)
                pool.wait_ge(ln_a[0], 4)
                nc.gpsimd.tensor_tensor(early_parts[:, :, 2, :], sq_all[0], early_parts[:, :, 1, :], ALU.subtract
                                        ).then_inc(h_ready[0], 1)
                pool.wait_ge(h_ready[0], 1)
                pool.wait_ge(h_ready[1], 1)

                def base(turn):
                    wait_apart(pool, x_landed, turn * 16 + 16)
                    if not first(turn):
                        pool.wait_ge(centred, done(turn))
                        wait_apart(pool, x1_stored, turn * 16)
                    hp = h_parts[:, bass.ds(turn * SUP, SUP), :, :]
                    for c in range(3):
                        ins = nc.gpsimd.tensor_tensor(x1_sup, x_sup if c == 0 else x1_sup, hp[:, :, c, :], ALU.add)
                        link(ins)
                    pool.sem_inc(base_built, 1)

                def add_sum(turn, r):
                    pool.wait_ge(sum_copied, done(turn * NB + r + 1))
                    a = l0_sum[:, r % 2, :, :]
                    link(nc.gpsimd.tensor_tensor(a[:, 1, :], a[:, 1, :], a[:, 2, :], ALU.add))
                    link(nc.gpsimd.tensor_tensor(a[:, 0, :], a[:, 0, :], a[:, 1, :], ALU.add))
                    xb = x1_sup[:, r, :]
                    nc.gpsimd.tensor_tensor(xb, xb, a[:, 0, :], ALU.add).then_inc(sum_added, 1)

                def build(sup):
                    pool.wait_ge(exp_ready, done(sup + 1))
                    for g in range(2):
                        last = nc.gpsimd.tensor_tensor(g_full[:, g], wh, exps[:, g, :].unsqueeze(2).broadcast_to(
                            [P, SUP, DE]), ALU.mult)
                    link(last)
                    gp = gparts[:, bass.ds(sup * SUP, SUP), :, :, :].rearrange("p t g c d -> p g t c d")
                    for c in range(2):
                        for g in range(2):
                            last = nc.gpsimd.tensor_copy(gp[:, g, :, c, :], g_full[:, g])
                        link(last)
                        for g in range(2):
                            to = g_full[:, g] if c == 0 else gp[:, g, :, 2, :]
                            last = nc.gpsimd.tensor_tensor(to, g_full[:, g], gp[:, g, :, c, :], ALU.subtract)
                        link(last)
                    nc.gpsimd.tensor_tensor(wh_sum, wh_sum, wh[:, :, 0:D], ALU.add).then_inc(g_built, 1)

                def add_pair(sup, j):
                    u = sup * 2 + j
                    pool.wait_ge(pair_copied, done(u + 1))
                    nc.gpsimd.tensor_tensor(pair_acc[:, :, 1, :], pair_acc[:, :, 1, :], pair_acc[:, :, 2, :], ALU.add
                                            ).then_inc(pair_chain, 1)
                    wait_apart(pool, pair_chain, u + 1)
                    wait_apart(pool, pair_stored, u * 16 + 16)
                    nc.gpsimd.tensor_tensor(pair_sums, pair_acc[:, :, 0, :], pair_acc[:, :, 1, :], ALU.add
                                            ).then_inc(pair_added, 1)

                def add_pairs(pairs, r):
                    for n, (sup, j) in enumerate(pairs):
                        if r == ADD_AT[n]:
                            add_pair(sup, j)

                def between():
                    pool.wait_ge(pair_stored, 2 * NE * 16 + 16)

                LINKS = 3 + 2 * NB + 5
                count = [0]

                def body(turn, pairs=()):
                    if not isinstance(turn, int):
                        chain.n = turn * LINKS + (count[0] - LINKS)
                    elif turn:
                        chain.n = count[0] + (TURNS - 2) * LINKS
                    base(turn)
                    for r in range(NB):
                        add_sum(turn, r)
                        add_pairs(pairs, r)
                        if r == (3 if last_turn(turn) else 2) and not first(turn):
                            build(turn - 1)
                    if first(turn):
                        count[0] = chain.n

                turns(pool, body, between)
                build(NS - 1)
                pool.wait_ge(d_abs_ready, 1)
                nc.gpsimd.partition_all_reduce(d_abs[:, 1:2], d_abs[:, 0:1], P, RMAX).then_inc(d_all_ready, 1)

        fin = sb("fin", [P, SUP, 3], F32)

        PAIRS1, PAIRS0 = (NE - 2) // 2, (NE + 1) // 2

        def lo_of(s):
            return int(s < NE)

        def superblocks(eng, body):
            with eng.Fori(0, PAIRS1) as pair:
                for par in range(2):
                    body(pair * 2 + par, par, 1, 1, 1)
            for s in range(2 * PAIRS1, 2 * PAIRS0):
                body(s, s % 2, lo_of(s), lo_of(s + 1), lo_of(s + 2))
            with eng.Fori(PAIRS0, NS // 2 - 1) as pair:
                for par in range(2):
                    body(pair * 2 + par, par, 0, 0, 0)
            body(NS - 2, 0, 0, 0, None)

        with nc.Block() as block:
            @block.sync
            def _(sp):
                general = sp.value_load(flag[0:1, 0:1], min_val=0, max_val=1)
                with sp.If(general == 0):
                    def load_x1(s, par):
                        sp.dma_start(x1_back[:, par], x1_sups[s]).then_inc(x1_in[par], 16)

                    def load_partial(s, par):
                        sp.dma_start(partial_back[:, par], partial_dram[s]).then_inc(partial_in[par], 16)

                    def rows(s, par, lo, more=True, partial=False):
                        if more:
                            v, _ = order(s, par, NCH - 1, lo)
                            sp.wait_ge(signs_ready, done(v * 2 + 2))
                            load_s(sp, s + 2, par)
                        sp.wait_ge(rows_out, done(s + 1))
                        sp.dma_start(out_rows[s], x1_back[:, par]).then_inc(out_done, 16)
                        if partial:
                            load_partial(s + 2, par)
                        if more:
                            sp.wait_ge(out_done, s * 16 + 16)
                            load_x1(s + 2, par)

                    for par in range(2):
                        load_x1(par, par)
                        load_partial(par, par)
                    with sp.Fori(0, PAIRS1) as pair:
                        for par in range(2):
                            rows(pair * 2 + par, par, 1, partial=True)
                    for s in range(2 * PAIRS1, 2 * PAIRS0):
                        rows(s, s % 2, lo_of(s), partial=lo_of(s + 2))
                    with sp.Fori(PAIRS0, NS // 2 - 1) as pair:
                        for par in range(2):
                            rows(pair * 2 + par, par, 0)
                    for par in range(2):
                        rows(NS - 2 + par, par, 0, more=False)
                with sp.Else():
                    sp.dma_start(s_rows_all, s_dram.broadcast_to([P, N])).then_inc(gen_in, 16)
                    for k in range(NS):
                        sp.dma_start(wh_all[:, k * SUP:(k + 1) * SUP, 0:D], wh_sups[k]).then_inc(gen_in, 16)
                    sp.dma_start(x1_all.rearrange("p (s b) d -> p s (b d)", b=SUP), x1_dram.rearrange("s q n -> q s n")
                                 ).then_inc(gen_in, 16)
                    with sp.Fori(0, NS) as s:
                        sp.wait_ge(gen_rows, done(s * SUP + SUP))
                        sp.dma_start(out_rows[s], x1_all[:, bass.ds(s * SUP, SUP), :]).then_inc(out_done, 16)
                sp.wait_ge(out_done, 16 * NS)

            @block.scalar
            def _(act):
                general = act.value_load(flag[0:1, 0:1], min_val=0, max_val=1)
                with act.If(general == 0):
                    def copy_first(s, par, lo):
                        v, _ = order(s, par, NCH - 1, lo)
                        act.wait_ge(chunk_done, done(v + 1))
                        act.wait_ge(rows_out, done(s))
                        src = psum[:, 4 * par:4 * par + SUP, 0:6 * DE].rearrange("p b (g c d) -> p b g c d", g=2, c=3)
                        for g in range(2):
                            last = nc.scalar.activation(sums[:, :, g, :], src[:, :, g, 0, :], ACT.Copy)
                        last.then_inc(first_copied, 1)

                    def body(s, par, lo, lo1, lo2):
                        for h in range(2 * lo1 + 4, NH):
                            signs(act, s + 1, 1 - par, h, lo1)
                            if h == 2 * lo1 + 4:
                                copy_first(s, par, lo)
                        for h in range(2 * lo2, 2 * lo2 + 4) if lo2 is not None else ():
                            signs(act, s + 2, par, h, lo2)

                    act.wait_ge(factors_in, 1)
                    nc.scalar.activation(factors, factors, ACT.Exp).then_inc(factors_ready, 1)
                    superblocks(act, body)
                    copy_first(NS - 1, 1, 0)
                with act.Else():
                    with act.Fori(0, T) as b:
                        act.wait_ge(gen_z, b + 1)
                        nc.scalar.activation(z_all, z_all, ACT.Exp).then_inc(gen_exp, 1)

            @block.vector
            def _(dve):
                general = dve.value_load(flag[0:1, 0:1], min_val=0, max_val=1)
                with dve.If(general == 0):
                    dve.sem_inc(rows_out, HEAD)
                    dve.sem_inc(sums_ready, HEAD)
                    nc.vector.tensor_scalar(factors[:, :, 0], s_col[:, :], 0.0, 1.0 - SLOPE, ALU.min, ALU.mult)
                    nc.vector.tensor_scalar(factors[:, :, 1], s_col[:, :], 0.0, SLOPE - 1.0, ALU.max, ALU.mult
                                            ).then_inc(factors_in, 1)
                    STEPS = 10

                    def finish(s, par, lo):
                        count = [0]

                        def link(ins):
                            count[0] += 1
                            ins.then_inc(l1_v, 1)
                            dve.wait_ge(l1_v, (s * (STEPS + 1) if lo else s * STEPS + NE) + count[0])

                        src = psum[:, 4 * par:4 * par + SUP, 0:6 * DE].rearrange("p b (g c d) -> p b g c d", g=2, c=3)
                        dve.wait_ge(first_copied, done(s + 1))
                        for c in (1, 2):
                            for g in range(2):
                                last = nc.vector.tensor_tensor(sums[:, :, g, :], sums[:, :, g, :], src[:, :, g, c, :],
                                                               ALU.add)
                            link(last)
                        dve.sem_inc(sums_ready, 1)
                        if lo:
                            dve.wait_ge(partial_in[par], (s - par) * 8 + 16)
                            link(nc.vector.tensor_tensor(
                                sums.rearrange("p b g d -> p (b g d)"), sums.rearrange("p b g d -> p (b g d)"),
                                partial_back[:, par], ALU.add))
                        dve.wait_ge(factors_ready, 1)
                        for g in range(2):
                            last = nc.vector.tensor_tensor(
                                sums[:, :, g, :], sums[:, :, g, :],
                                factors[:, bass.ds(s * SUP, SUP), g].unsqueeze(2).broadcast_to([P, SUP, DE]), ALU.mult)
                        link(last)
                        num = sums[:, :, 0, :]
                        link(nc.vector.tensor_tensor(num, num, sums[:, :, 1, :], ALU.add))
                        link(nc.vector.tensor_scalar(fin[:, :, 0], num[:, :, D], 0.0, None, ALU.is_equal))
                        link(nc.vector.tensor_tensor(fin[:, :, 1], num[:, :, D], fin[:, :, 0], ALU.add))
                        nc.vector.reciprocal(fin[:, :, 2], fin[:, :, 1])
                        link(nc.vector.tensor_tensor(
                            sums[:, :, 1, 0:D], wh_mean[:, :].unsqueeze(1).broadcast_to([P, SUP, D]),
                            fin[:, :, 0].unsqueeze(2).broadcast_to([P, SUP, D]), ALU.mult))
                        link(nc.vector.tensor_tensor(num[:, :, 0:D], num[:, :, 0:D], sums[:, :, 1, 0:D], ALU.add))
                        link(nc.vector.tensor_tensor(num[:, :, 0:D], num[:, :, 0:D],
                                                     fin[:, :, 2].unsqueeze(2).broadcast_to([P, SUP, D]), ALU.mult))
                        xb = x1_back[:, par]
                        dve.wait_ge(biased, s + 1)
                        link(nc.vector.tensor_tensor(xb, xb, num[:, :, 0:D], ALU.add))
                        dve.sem_inc(rows_out, 1)
                        assert count[0] == STEPS + lo

                    def body(s, par, lo, lo1, lo2):
                        for c in range(lo1 + 2, NCH):
                            chunk(dve, s + 1, 1 - par, c, lo1)
                            if c == lo1 + 2:
                                finish(s, par, lo)
                        for c in range(lo2, lo2 + 2) if lo2 is not None else ():
                            chunk(dve, s + 2, par, c, lo2)

                    superblocks(dve, body)
                    finish(NS - 1, 1, 0)
                with dve.Else():
                    dve.sem_inc(gen_rows, HEAD)
                    STEPS = 19
                    w_view = words[:, :, :, :, :]
                    dve.wait_ge(gen_in, (NS + 2) * 16)
                    nc.vector.memset(wh_all[:, :, D:DE], 1.0)
                    nc.vector.tensor_tensor(x1_all, x1_all, bias_b[:, :].unsqueeze(1).broadcast_to([P, T, D]),
                                            ALU.add).then_inc(gen_v, 1)
                    dve.wait_ge(gen_v, 1)
                    with dve.Fori(0, NS) as s:
                        for k in range(SUP):
                            b = s * SUP + k
                            count = [0]

                            def link(ins):
                                count[0] += 1
                                ins.then_inc(gen_v, 1)
                                wait_apart(dve, gen_v, b * STEPS + count[0] + 1)

                            e16 = edges1.rearrange("p t i -> p (t i)").bitcast(U16).rearrange(
                                "p (n m w) -> p n m w", m=8, w=W1)
                            w16 = w_view[:, s, :, k, :].bitcast(U16)
                            dve.wait_ge(gen_rows, done(b))
                            link(spread(dve, [e16[:, :, m, :] for m in range(8)], w16))
                            e8 = edges1.bitcast(FP8)
                            link(nc.vector.tensor_scalar(tmp, d_col[:, :], d_abs[:, 1:2], None, ALU.add))
                            link(nc.vector.tensor_tensor(z_all, e8, tmp.unsqueeze(2).broadcast_to([P, T, P]), ALU.mult))
                            link(nc.vector.tensor_reduce(out=row_max, in_=z_all.rearrange("p t i -> p i t"),
                                                         axis=AXX, op=ALU.max))
                            dve.sem_inc(gen_max, 1)
                            dve.wait_ge(gen_turned, b + 1)
                            link(nc.vector.tensor_reduce(out=m_cols[:, 0:1], in_=psum[:, 0, 0:P], axis=AXX, op=ALU.max))
                            link(nc.vector.tensor_scalar(m_cols[:, 0:1], m_cols[:, 0:1], 0.5, d_abs[:, 1:2],
                                                         ALU.mult, ALU.subtract))
                            link(nc.vector.tensor_tensor(m_cols[:, 0:1], m_cols[:, 0:1], s_col[:, bass.ds(b, 1)], ALU.add))
                            link(nc.vector.scalar_tensor_tensor(out=m_cols[:, 1:2], in0=m_cols[:, 0:1], scalar=SLOPE,
                                                                in1=m_cols[:, 0:1], op0=ALU.mult, op1=ALU.max))
                            link(nc.vector.tensor_scalar(m_diag, ident[:, :], m_cols[:, 1:2], None, ALU.mult))
                            dve.sem_inc(gen_mdiag, 1)
                            link(nc.vector.tensor_tensor(
                                z_all, s_rows_all[:, bass.ds(b * P, P)].unsqueeze(1).broadcast_to([P, T, P]),
                                d_col[:, :].unsqueeze(2).broadcast_to([P, T, P]), ALU.add))
                            link(nc.vector.scalar_tensor_tensor(out=z_all, in0=z_all, scalar=SLOPE, in1=z_all,
                                                                op0=ALU.mult, op1=ALU.max))
                            dve.wait_ge(gen_m, b + 1)
                            link(nc.vector.tensor_tensor(
                                z_all, z_all, psum[:, 1, 0:P].unsqueeze(1).broadcast_to([P, T, P]), ALU.subtract))
                            link(nc.vector.tensor_scalar(z_all, z_all, 0.0, None, ALU.min))
                            dve.sem_inc(gen_z, 1)
                            wait_apart(dve, gen_exp, b + 1)
                            link(nc.vector.tensor_tensor(z_all, z_all, e8, ALU.mult))
                            dve.sem_inc(gen_e, 1)
                            dve.wait_ge(gen_sum, b + 1)
                            link(nc.vector.tensor_copy(out1, psum[:, 2, 0:DE]))
                            link(nc.vector.tensor_scalar(m_cols[:, 2:3], out1[:, D:DE], 0.0, None, ALU.is_equal))
                            link(nc.vector.scalar_tensor_tensor(out=out1[:, 0:D], in0=wh_mean[:, :], scalar=m_cols[:, 2:3],
                                                                in1=out1[:, 0:D], op0=ALU.mult, op1=ALU.add))
                            link(nc.vector.tensor_tensor(out1[:, D:DE], out1[:, D:DE], m_cols[:, 2:3], ALU.add))
                            link(nc.vector.reciprocal(m_cols[:, 3:4], out1[:, D:DE]))
                            xb = x1_all[:, b, :]
                            nc.vector.scalar_tensor_tensor(out=xb, in0=out1[:, 0:D], scalar=m_cols[:, 3:4], in1=xb,
                                                           op0=ALU.mult, op1=ALU.add).then_inc(gen_rows, 1)
                            assert count[0] == STEPS

            @block.tensor
            def _(pe):
                general = pe.value_load(flag[0:1, 0:1], min_val=0, max_val=1)
                with pe.If(general == 0):
                    def body(s, par, lo, lo1, lo2):
                        for h in range(2 * lo1 + 2, NH):
                            multiply1(pe, s + 1, 1 - par, h, lo1)
                        if lo2 is not None:
                            pe.wait_ge(sums_ready, done(s + 1))
                            for h in range(2 * lo2, 2 * lo2 + 2):
                                multiply1(pe, s + 2, par, h, lo2)

                    superblocks(pe, body)
                with pe.Else():
                    with pe.Fori(0, T) as b:
                        pe.wait_ge(gen_max, b + 1)
                        nc.tensor.transpose(psum[:, 0, 0:P], row_max, ident[:, :]).then_inc(gen_turned, 1)
                        pe.wait_ge(gen_mdiag, b + 1)
                        nc.tensor.matmul(psum[:, 1, 0:P], ones[:, :], m_diag, start=True, stop=True).then_inc(gen_m, 1)
                        pe.wait_ge(gen_e, b + 1)
                        for t in range(T):
                            last = nc.tensor.matmul(psum[:, 2, 0:DE], z_all[:, t, :], wh_all[:, t, :],
                                                    start=(t == 0), stop=(t == T - 1))
                        last.then_inc(gen_sum, 1)

            @block.gpsimd
            def _(pool):
                general = pool.value_load(flag[0:1, 0:1], min_val=0, max_val=1)
                with pool.If(general == 0):
                    with pool.Fori(0, NS // 2) as pair:
                        for par in range(2):
                            s = pair * 2 + par
                            wait_apart(pool, x1_in[par], pair * 16 + 16)
                            xb = x1_back[:, par]
                            nc.gpsimd.tensor_tensor(xb, xb, bias_b[:, :].unsqueeze(1).broadcast_to([P, SUP, D]),
                                                    ALU.add).then_inc(biased, 1)


def kernel(x, adj, L1_gnn_weight_w, L1_gnn_weight_a, L1_gnn_bias):
    import numpy as np
    import concourse.bacc as bacc
    from concourse.bass_utils import run_bass_kernel_spmd

    nc = bacc.Bacc("TRN2", target_bir_lowering=False, num_devices=1)
    arrays, args = {}, []
    for name, a in (("x", x), ("adj", adj), ("weight_w", L1_gnn_weight_w),
                    ("weight_a", L1_gnn_weight_a), ("bias", L1_gnn_bias)):
        a = np.ascontiguousarray(a)
        arrays[name] = a
        args.append(nc.dram_tensor(name, a.shape, mybir.dt.from_np(a.dtype), kind="ExternalInput").ap())
    args.append(nc.dram_tensor("out", x.shape, mybir.dt.float32, kind="ExternalOutput").ap())
    gnn_two_layers(nc, *args)
    r = run_bass_kernel_spmd(nc, [arrays], core_ids=[0])
    return r.results[0]["out"]
```
